# Optimizing a Trainium2 kernel written in Bass

```python
import numpy as np
import jax
import jax.numpy as jnp

def _softmax(x, axis=-1):
    return jax.nn.softmax(x, axis=axis)

def _gelu(x):
    return jax.nn.gelu(x, approximate=True)

def _silu(x):
    return jax.nn.silu(x)

def _sigmoid(x):
    return jax.nn.sigmoid(x)

def _layernorm(x, axis=-1, eps=1e-05):
    m = jnp.mean(x, axis=axis, keepdims=True)
    v = jnp.var(x, axis=axis, keepdims=True)
    return (x - m) / jnp.sqrt(v + eps)

def _scatter_add(tgt, idx, src, axis=0):
    return tgt.at[idx].add(src)

def _segment_sum(src, seg, n):
    return jax.ops.segment_sum(src, seg, n)
kernel_name = 'mk_cond_resid_d1_seqx_r2_e96b3f'

def setup_inputs(seed: int=0):
    np.random.seed(seed)
    _w = jnp.asarray

    def _rec_inputs():
        import jax
        import jax.numpy as jnp
        _rk = jax.random.key(seed)
        x = -0.0003929 + 0.9999 * jax.random.normal(jax.random.fold_in(_rk, 1), (128, 128, 512), jnp.float32)
        _lenS = 128 - jax.random.randint(jax.random.fold_in(_rk, 7), (128,), 0, max(1, 128 // 4) + 1, jnp.int32)
        _lenS2 = 128 - jax.random.randint(jax.random.fold_in(_rk, 8), (128,), 0, max(1, 128 // 4) + 1, jnp.int32)
        cond_2048 = 0.00782532 + 1.00527 * jax.random.normal(jax.random.fold_in(_rk, 11), (128, 1024), jnp.float32)
        return (x, cond_2048)
    x, cond_2048 = _rec_inputs()

    def _L0_cond_setup():
        import jax, jax.numpy as jnp
        import numpy as np
        B, S, D_MODEL, D_INNER, D_STATE = (4, 2048, 512, 1024, 16)
        key = jax.random.key(seed)
        ks = jax.random.split(key, 12)
        inp = {'x': jax.random.normal(ks[0], (B, S, D_MODEL), jnp.float32), 't_emb': jax.random.normal(ks[1], (B, D_INNER), jnp.float32), 'W_in': jax.random.normal(ks[2], (2 * D_INNER, D_MODEL), jnp.float32) * 0.02, 'W_conv': jax.random.normal(ks[3], (D_INNER, 1, 4), jnp.float32) * 0.1, 'b_conv': jnp.zeros((D_INNER,), jnp.float32), 'ln_g': jnp.ones((D_INNER,), jnp.float32), 'ln_b': jnp.zeros((D_INNER,), jnp.float32), 'W_xproj': jax.random.normal(ks[4], (3 * D_STATE, D_INNER), jnp.float32) * 0.02, 'W_dt': jax.random.normal(ks[5], (D_STATE, D_STATE), jnp.float32) * 0.01, 'b_dt': jax.random.uniform(ks[6], (D_STATE,), jnp.float32) * 0.1, 'A_log': jax.random.normal(ks[7], (D_STATE,), jnp.float32) * 0.1, 'D': jnp.ones((D_INNER,), jnp.float32) * 0.1, 'W_out': jax.random.normal(ks[8], (D_MODEL, D_INNER), jnp.float32) * 0.02}
        return inp
    _L0_cond_all = _L0_cond_setup()
    _L0_cond_in = {k: v for k, v in _L0_cond_all.items() if k in ('W_in', 'W_conv', 'b_conv', 'ln_g', 'ln_b', 'W_xproj', 'W_dt', 'b_dt', 'A_log', 'D', 'W_out')}
    del _L0_cond_all
    return {'x': x, 'cond_2048': cond_2048, 'L0_cond_W_in': _L0_cond_in['W_in'], 'L0_cond_W_conv': _L0_cond_in['W_conv'], 'L0_cond_b_conv': _L0_cond_in['b_conv'], 'L0_cond_ln_g': _L0_cond_in['ln_g'], 'L0_cond_ln_b': _L0_cond_in['ln_b'], 'L0_cond_W_xproj': _L0_cond_in['W_xproj'], 'L0_cond_W_dt': _L0_cond_in['W_dt'], 'L0_cond_b_dt': _L0_cond_in['b_dt'], 'L0_cond_A_log': _L0_cond_in['A_log'], 'L0_cond_D': _L0_cond_in['D'], 'L0_cond_W_out': _L0_cond_in['W_out']}

def reference(x, cond_2048, L0_cond_W_in, L0_cond_W_conv, L0_cond_b_conv, L0_cond_ln_g, L0_cond_ln_b, L0_cond_W_xproj, L0_cond_W_dt, L0_cond_b_dt, L0_cond_A_log, L0_cond_D, L0_cond_W_out):
    import jax
    import jax.numpy as jnp

    def _L0_cond_ref(x, t_emb, W_in, W_conv, b_conv, ln_g, ln_b, W_xproj, W_dt, b_dt, A_log, D, W_out):
        import jax, jax.numpy as jnp
        import numpy as np
        B, S, D_MODEL, D_INNER, D_STATE = (4, 2048, 512, 1024, 16)
        d_inner = W_conv.shape[0]
        d_state = A_log.shape[0]
        xr, gate = jnp.split(x @ W_in.T, 2, axis=-1)
        xr = xr + t_emb[:, None, :]
        xc = jax.lax.conv_general_dilated(xr.transpose(0, 2, 1), W_conv, (1,), [(3, 0)], feature_group_count=d_inner, dimension_numbers=('NCH', 'OIH', 'NCH')) + b_conv[None, :, None]
        xc = jax.nn.silu(xc).transpose(0, 2, 1)
        mu = xc.mean(-1, keepdims=True)
        var = xc.var(-1, keepdims=True)
        xn = (xc - mu) / jnp.sqrt(var + 1e-05) * ln_g + ln_b
        Bm, Cm, dt = jnp.split(xn @ W_xproj.T, 3, axis=-1)
        dt = jnp.tanh(dt @ W_dt.T + b_dt) * 0.01
        A = -jnp.tanh(A_log)
        Ad = 1.0 + dt * A
        Bd = Bm * jnp.minimum(jnp.linalg.norm(xn, axis=-1, keepdims=True), 1.0)
        h0 = jnp.zeros((xn.shape[0], d_state, d_inner), xn.dtype)

        def step(h, inputs):
            ad, bd, xt, ct = inputs
            h = jnp.clip(h * ad[:, :, None] + bd[:, :, None] * xt[:, None, :], -10.0, 10.0)
            yt = jnp.einsum('bd,bdh->bh', ct, h)
            return (h, yt)
        _, ys = jax.lax.scan(step, h0, (Ad.transpose(1, 0, 2), Bd.transpose(1, 0, 2), xn.transpose(1, 0, 2), Cm.transpose(1, 0, 2)))
        y = ys.transpose(1, 0, 2) + D * xn
        return y * jax.nn.silu(gate) @ W_out.T
    x = x + _L0_cond_ref(x, cond_2048, L0_cond_W_in, L0_cond_W_conv, L0_cond_b_conv, L0_cond_ln_g, L0_cond_ln_b, L0_cond_W_xproj, L0_cond_W_dt, L0_cond_b_dt, L0_cond_A_log, L0_cond_D, L0_cond_W_out)
    return x

_drawn_inputs = setup_inputs


def setup_inputs(seed=0):
    import zlib

    import numpy as np

    out = dict(_drawn_inputs(seed))
    spreads = {'L0_cond_b_conv': (0.0, 0.1),
     'L0_cond_ln_g': (1.0, 0.2),
     'L0_cond_ln_b': (0.0, 0.1),
     'L0_cond_D': (0.10000000149011612, 0.6)}
    factors = {'L0_cond_W_dt': 34.564, 'L0_cond_b_dt': 27.367, 'L0_cond_A_log': 8.0}
    for name, (base, spread) in spreads.items():
        noise = np.random.default_rng([zlib.crc32(name.encode()), seed]).standard_normal(out[name].shape)
        drawn = base * np.exp(spread * noise) if base else spread * noise
        out[name] = jnp.asarray(drawn.astype(out[name].dtype))
    for name, factor in factors.items():
        out[name] = (out[name] * factor).astype(out[name].dtype)
    return out
```

```python
from contextlib import ExitStack

import concourse.bass as bass
from concourse import mybir

F32 = mybir.dt.float32
F32R = mybir.dt.float32r
BF16 = mybir.dt.bfloat16
ALU = mybir.AluOpType
ACT = mybir.ActivationFunctionType
AX_X = mybir.AxisListType.X

P = 128
BATCH, SEQ, DM, DI, DS = 128, 128, 512, 1024, 16
NB, TS, NG = 8, 4, 4
BSET = NG * NB
SETS = BATCH // BSET
TPC = 2
CH = TPC * P
CPS = SEQ // (TS * TPC)
CHUNKS = SETS * CPS
TILES = CHUNKS * TPC
KD = DM // P
KI = DI // P
HALF = 512
ITEMS = TS * NG
TAPS = 4
CLIP = 10.0
EPS = 1e-5
NPROJ = 3 * DS

BEFORE = {0: ["xr0", "xr1", "xr2", "xr3", "tr0.1", "xp.1", "sm.1"], 1: ["tr1.1", "ga0.1", "ga1.1"]}
BODY = {
    0: ["xr0", "xr1", "xr2", "xr3", "ga1.0", "tr0.1", "xp.1", "ot0.1", "sm.1"],
    1: ["tr0.0", "tr1.0", "xp.0", "ga0.0", "ot0.0", "ot1.0", "ou.0", "sm.0",
        "tr1.1", "ga0.1", "ot1.1", "ou.1", "ga1.1"],
}
AFTER = {0: [], 1: ["ot0.0", "ot1.0", "ou.0"]}


def bank_use(name, c, back=0):
    last = isinstance(c, int) and c == CHUNKS and back == 0
    for bank in (0, 1):
        order = BEFORE[bank] if c is None else AFTER[bank] if last else BODY[bank]
        if name in order:
            if c is None:
                return bank, order.index(name)
            return bank, c * len(BODY[bank]) + (len(BEFORE[bank]) + order.index(name) - back * len(BODY[bank]))
    raise KeyError(name)


def build(nc, xT, xtok, temb, w_in, w_conv, b_conv, ln_g, ln_b, g_rows, b_rows, d_rows, w_x, w_x3,
          w_dt, b_dt, a_log, w_out, ident, sel, mask, out):
    with ExitStack() as ctx:
        def sb(name, shape, dt=F32):
            return ctx.enter_context(nc.sbuf_tensor(name, shape, dt))

        def psum(name, shape):
            return ctx.enter_context(nc.psum_tensor(name, shape, F32))

        def sem(name):
            return ctx.enter_context(nc.semaphore(name))

        win = sb("win", [P, KD, 2 * DI])
        wout = sb("wout", [P, KI, DM])
        wxg = sb("wxg", [P, KI, NPROJ])
        wc = sb("wc", [P, KI, TAPS])
        wneg = sb("wneg", [P, KI, TAPS])
        wsum = sb("wsum", [P, KI])
        bc = sb("bc", [P, KI])
        gcol = sb("gcol", [P, KI])
        bcol = sb("bcol", [P, KI])
        grow = sb("grow", [P, DI])
        brow = sb("brow", [P, DI])
        drow = sb("drow", [P, DI])
        tembs = sb("tembs", [P, SETS + 1, KI, BSET])
        idn = sb("idn", [P, P])
        selr = sb("selr", [P, 8, P], F32R)
        msk = sb("msk", [P, NB])
        s1 = sb("s1", [P, NPROJ])
        s2 = sb("s2", [P, NPROJ])
        a2 = sb("a2", [P, DS])
        expo = sb("expo", [P, 2])
        wx3 = sb("wx3", [DS, DI])
        wdt = sb("wdt", [DS, DS])
        xt = sb("xt", [P, KD, CH])
        xg = sb("xg", [P, KD, P])
        taps = [sb(f"taps{s}", [P, KI, NG, NB * (s + TS * TPC)]) for s in range(TAPS)]
        cterm = sb("cterm", [P, KI, BSET])
        halo = sb("halo", [P, KI, BSET])
        xct = [sb(f"xct{p}", [P, KI, P]) for p in range(2)]
        xn = [sb(f"xn{p}", [P, DI]) for p in range(2)]
        xhi = sb("xhi", [P, DI], F32R)
        sqj = sb("sqj", [P, DI], BF16)
        stack = [sb(f"stack{p}", [P, 2, DI], F32R) for p in range(2)]
        dx = [sb(f"dx{p}", [P, DI]) for p in range(2)]
        sg = [sb(f"sg{p}", [P, DI]) for p in range(2)]
        bst = sb("bst", [P, 2, 6])
        mv = sb("mv", [P, 2])
        ve = sb("ve", [P, 1])
        rstd = sb("rstd", [P, 1])
        nmr = sb("nmr", [P, 1])
        t48 = sb("t48", [P, NPROJ])
        q48 = sb("q48", [P, NPROJ])
        th = sb("th", [P, DS])
        ta = sb("ta", [P, DS])
        nsq = sb("nsq", [P, 1])
        nmin = sb("nmin", [P, 1])
        nrm = sb("nrm", [P, 1])
        x3 = sb("x3", [P, 3, P])
        ba = sb("ba", [P, 2, ITEMS])
        pcar = sb("pcar", [P, NG])
        pp = [sb(f"pp{p}", [P, NG, TS]) for p in range(2)]
        ip = sb("ip", [P, ITEMS])
        lim = [sb(f"lim{p}", [P, 2, ITEMS]) for p in range(2)]
        bdp = [sb(f"bdp{p}", [P, ITEMS]) for p in range(2)]
        lhc = [sb(f"lhc{p}", [P, NG, TS, BSET]) for p in range(2)]
        st = [sb(f"st{p}", [P, NG, DI]) for p in range(2)]
        ygt = sb("ygt", [P, KI, P])
        res = sb("res", [P, DM])

        px = [psum(f"px{p}", [P, DI]) for p in range(2)]
        py = psum("py", [P, DI])
        wb = [psum(f"wb{p}", [P, HALF]) for p in range(2)]

        loaded = sem("loaded")
        setup_v = sem("setup_v")
        setup_t = sem("setup_t")
        setup_a = sem("setup_a")
        setup_raw = sem("setup_raw")
        xt_loaded = sem("xt_loaded")
        xg_loaded = sem("xg_loaded")
        bank_ready = [sem(f"bank_ready{p}") for p in range(2)]
        bank_free = [sem(f"bank_free{p}") for p in range(2)]
        conv_step = sem("conv_step")
        conv_done = sem("conv_done")
        set_step = sem("set_step")
        silu_done = sem("silu_done")
        stat_step = sem("stat_step")
        ve_done = sem("ve_done")
        rstd_done = sem("rstd_done")
        xhat_done = sem("xhat_done")
        aff_step = sem("aff_step")
        xn_done = sem("xn_done")
        th_done = sem("th_done")
        nsq_done = sem("nsq_done")
        nmin_done = sem("nmin_done")
        nrm_done = sem("nrm_done")
        hi_done = sem("hi_done")
        dx_done = sem("dx_done")
        lo_done = sem("lo_done")
        stacked = sem("stacked")
        x3_step = sem("x3_step")
        x3_done = sem("x3_done")
        coef_step = sem("coef_step")
        coef_done = sem("coef_done")
        x_done = sem("x_done")
        upd_done = sem("upd_done")
        clip_done = sem("clip_done")
        y_done = sem("y_done")
        state_zero = sem("state_zero")
        decay_reset = sem("decay_reset")
        evac_done = sem("evac_done")
        yg_done = sem("yg_done")
        res_loaded = sem("res_loaded")
        stored = sem("stored")

        UPD0 = 2
        CLIP0 = 4
        Y0 = 2
        STORED0 = 16

        def apart(eng):
            eng.nop(nofuse=True)

        def vacant(name, c):
            bank, before = bank_use(name, c)
            return bank_free[bank], before

        def filled(name, c):
            bank, before = bank_use(name, c)
            return bank_ready[bank], before + 1

        def read_out(name, c, back=0):
            bank, before = bank_use(name, c, back)
            return bank_free[bank], before + 1

        LOADS = 18

        block = ctx.enter_context(nc.Block())

        @block.sync
        def _(sp):
            for dst, src in ((idn, ident), (wx3, w_x3), (wdt, w_dt), (wc, w_conv), (bc, b_conv), (gcol, ln_g),
                             (bcol, ln_b), (wxg, w_x), (s2, b_dt), (a2, a_log), (msk, mask), (tembs, temb),
                             (win, w_in), (wout, w_out), (grow, g_rows), (brow, b_rows), (drow, d_rows),
                             (st[0][:, 0, :].rearrange("p (a b) -> p a b", a=8), sel)):
                sp.dma_start(dst[:], src).then_inc(loaded, 16)

            def load_chunk(f, c):
                if c is not None:
                    sp.wait_ge(*read_out("ga1.1", c, back=1))
                sp.wait_ge(xg_loaded, 16 * f)
                sp.dma_start(xt[:], xT[f]).then_inc(xt_loaded, 16)

            def copy_second_tile(f, c):
                sp.wait_ge(xt_loaded, 16 * f + 16)
                if c is not None:
                    sp.wait_ge(*read_out("ga1.0", c))
                sp.dma_start(xg[:], xt[:, :, P:CH]).then_inc(xg_loaded, 16)

            def stack_parts(U, p, c):
                sp.wait_ge(hi_done, U + 1)
                apart(sp)
                sp.wait_ge(lo_done, U + 1)
                apart(sp)
                if p == 1 or c is not None:
                    sp.wait_ge(x_done, ITEMS * (U - 1) + 1)
                hi, lo, st32 = xhi[:].bitcast(F32), xn[p], stack[p][:].bitcast(F32)
                for pair in range(2):
                    rows = slice(64 * pair, 64 * pair + 64)
                    sp.dma_start(st32[0:64, pair, :], hi[rows, :]).then_inc(stacked, 16)
                    sp.dma_start(st32[64:128, pair, :], lo[rows, :]).then_inc(stacked, 16)

            def load_residual(T):
                sp.wait_ge(stored, 16 * T + STORED0)
                sp.dma_start(res[:], xtok[T]).then_inc(res_loaded, 16)

            def store(T, j, c):
                sp.wait_ge(*read_out(f"ou.{j}", c))
                sp.dma_start(out[T], res[:]).then_inc(stored, 16)

            sp.sem_inc(stored, STORED0)
            load_chunk(0, None)
            copy_second_tile(0, None)
            stack_parts(0, 0, None)
            with sp.Fori(0, SETS) as s:
                with sp.Fori(0, CPS) as k:
                    c = s * CPS + k
                    load_chunk(c + 1, c)
                    load_residual(2 * c)
                    stack_parts(2 * c + 1, 1, c)
                    store(2 * c, 0, c)
                    copy_second_tile(c + 1, c)
                    load_residual(2 * c + 1)
                    stack_parts(2 * c + 2, 0, c)
                    store(2 * c + 1, 1, c)
            load_residual(TILES)
            store(TILES, 0, CHUNKS)
            sp.wait_ge(stored, 16 * (TILES + 1) + STORED0)

        @block.tensor
        def _(pe):
            def input_blocks(q, part, f, c):
                if part == 0:
                    pe.wait_ge(*vacant(f"xr{q}", c))
                    if q == 0:
                        pe.wait_ge(xt_loaded, 16 * f + 16)
                bank, _ = bank_use(f"xr{q}", c)
                blk = 2 * q + part
                for kd in range(KD):
                    mm = nc.tensor.matmul(wb[bank][:, part * CH:(part + 1) * CH], win[:, kd, blk * P:(blk + 1) * P],
                                          xt[:, kd, :], start=(kd == 0), stop=(kd == KD - 1))
                if part == 1:
                    mm.then_inc(bank_ready[bank], 1)

            def turn_xc(h, U, p, j, c):
                bank, _ = bank_use(f"tr{h}.{j}", c)
                ps = wb[bank]
                pe.wait_ge(*vacant(f"tr{h}.{j}", c))
                pe.wait_ge(silu_done, U + 1)
                for b in range(4):
                    mm = nc.tensor.transpose(ps[:, b * P:(b + 1) * P], xct[p][:, 4 * h + b, :], idn[:])
                mm.then_inc(bank_ready[bank], 1)

            def project_bcd(part, U, p, j, c):
                if part == 0:
                    pe.wait_ge(*vacant(f"xp.{j}", c))
                bank, _ = bank_use(f"xp.{j}", c)
                for blk in range(4 * part, 4 * part + 4):
                    mm = nc.tensor.matmul(wb[bank][:, 0:NPROJ], xct[p][:, blk, :], wxg[:, blk, :],
                                          start=(blk == 0), stop=(blk == KI - 1))
                if part == 1:
                    mm.then_inc(bank_ready[bank], 1)

            def gate(h, part, U, p, j, c):
                if part == 0:
                    pe.wait_ge(*vacant(f"ga{h}.{j}", c))
                    if j == 0:
                        pe.wait_ge(xg_loaded, 16 * (c + 1))
                bank, _ = bank_use(f"ga{h}.{j}", c)
                src = xt[:, :, 0:P] if j == 1 else xg
                for kd in (2 * part, 2 * part + 1):
                    mm = nc.tensor.matmul(wb[bank][:], src[:, kd, :],
                                          win[:, kd, DI + h * HALF:DI + (h + 1) * HALF], start=(kd == 0), stop=(kd == KD - 1))
                if part == 1:
                    mm.then_inc(bank_ready[bank], 1)

            def turn_coefs(U, j, c):
                bank, _ = bank_use(f"sm.{j}", c)
                ps = wb[bank]
                pe.wait_ge(*vacant(f"sm.{j}", c))
                pe.wait_ge(x3_done, U + 1)
                for v in range(3):
                    mm = nc.tensor.transpose(ps[:, v * P:(v + 1) * P], x3[:, v, :], idn[:])
                mm.then_inc(bank_ready[bank], 1)

            def spread(T, i, p):
                if i == 0:
                    pe.wait_ge(stacked, 64 * (T + 1))
                t, g = i // NG, i % NG
                pe.wait_ge(upd_done, ITEMS * T + i + 1 + UPD0 - 2)
                for h in range(2):
                    mm = nc.tensor.matmul(px[i % 2][:, h * HALF:(h + 1) * HALF], selr[:, (g % 2) * TS + t, :],
                                          stack[p][:, g // 2, h * HALF:(h + 1) * HALF], start=True, stop=True)
                mm.then_inc(x_done, 1)

            def contract(T, t, p):
                if t == 0:
                    pe.wait_ge(coef_done, T + 1)
                    pe.wait_ge(evac_done, T + 1)
                pe.wait_ge(clip_done, ITEMS * T + NG * t + NG + CLIP0)
                for h in range(2):
                    for g in range(NG):
                        mm = nc.tensor.matmul(py[g * BSET:(g + 1) * BSET, h * HALF:(h + 1) * HALF], lhc[p][:, g, t, :],
                                              st[t % 2][:, g, h * HALF:(h + 1) * HALF],
                                              start=(t == 0), stop=(t == TS - 1), tile_position=(0, g * BSET))
                mm.then_inc(y_done, 1)

            def turn_yg(h, T, j, c):
                bank, _ = bank_use(f"ot{h}.{j}", c)
                ps = wb[bank]
                pe.wait_ge(*vacant(f"ot{h}.{j}", c))
                pe.wait_ge(yg_done, T + 1)
                for b in range(4):
                    mm = nc.tensor.transpose(ps[:, b * P:(b + 1) * P], dx[1 - j][:, (4 * h + b) * P:(4 * h + b + 1) * P], idn[:])
                mm.then_inc(bank_ready[bank], 1)

            def project_out(part, T, j, c):
                if part == 0:
                    pe.wait_ge(*vacant(f"ou.{j}", c))
                    if j == 1:
                        pe.wait_ge(*read_out("ot0.1", c))
                bank, _ = bank_use(f"ou.{j}", c)
                for blk in (2 * part, 2 * part + 1):
                    mm = nc.tensor.matmul(wb[bank][:], ygt[:, blk, :], wout[:, blk, :], start=(blk == 0), stop=(blk == KI - 1))
                if part == 3:
                    mm.then_inc(bank_ready[bank], 1)

            pe.wait_ge(loaded, 16 * LOADS)
            for blk in range(KI):
                mm = nc.tensor.matmul(px[0][:, blk * DS:(blk + 1) * DS], wx3[:, blk * P:(blk + 1) * P], wdt[:],
                                      start=True, stop=True)
            mm.then_inc(setup_t, 1)
            pe.wait_ge(setup_v, 3)
            for blk in range(KI):
                nc.tensor.matmul(px[1][:, 0:NPROJ], st[1][:, 0, 0:P], wxg[:, blk, :], start=(blk == 0), stop=(blk == KI - 1))
            for blk in range(KI):
                mm = nc.tensor.matmul(px[1][:, HALF:HALF + NPROJ], st[1][:, 1, blk * P:(blk + 1) * P],
                                      st[1][:, 2, blk * NPROJ:(blk + 1) * NPROJ], start=(blk == 0), stop=(blk == KI - 1))
            mm.then_inc(setup_t, 1)

            def front(n, U, p, j, c):
                if n == 0:
                    turn_xc(0, U, p, j, c)
                if n == 1:
                    turn_xc(1, U, p, j, c)
                if n in (2, 3):
                    project_bcd(n - 2, U, p, j, c)
                if n in (4, 5):
                    gate(0, n - 4, U, p, j, c)
                if n == 12:
                    turn_coefs(U, j, c)
                if n in (13, 14):
                    gate(1, n - 13, U, p, j, c)

            for q in range(4):
                for part in range(2):
                    input_blocks(q, part, 0, None)
            pe.wait_ge(setup_v, SETUP_V)
            for n in range(ITEMS):
                front(n, 0, 0, 1, None)
            spread(0, 0, 0)
            spread(0, 1, 0)
            with pe.Fori(0, SETS) as s:
                with pe.Fori(0, CPS) as k:
                    c = s * CPS + k
                    for j in range(TPC):
                        T = 2 * c + j
                        for n in range(ITEMS):
                            if n + 2 < ITEMS:
                                spread(T, n + 2, j)
                            else:
                                spread(T + 1, n + 2 - ITEMS, 1 - j)
                            front(n, T + 1, 1 - j, j, c)
                            if j == 0 and 2 <= n < 10:
                                input_blocks((n - 2) // 2, n % 2, c + 1, c)
                            if n in (6, 7):
                                turn_yg(n - 6, T, j, c)
                            if 8 <= n < 12:
                                project_out(n - 8, T, j, c)
                            if n % NG == NG - 1:
                                contract(T, n // NG, j)
            for h in range(2):
                turn_yg(h, TILES, 0, CHUNKS)
            for part in range(4):
                project_out(part, TILES, 0, CHUNKS)

        @block.scalar
        def _(act):
            def scale_taps(q, f, c):
                bank, before = bank_use(f"xr{q}", c)
                act.wait_ge(bank_ready[bank], before + 1)
                if c is not None:
                    act.wait_ge(conv_done, 2 * f + q // 2 - 1)
                for part in range(2):
                    blk = 2 * q + part
                    src = wb[bank][:, part * CH:(part + 1) * CH].rearrange("p (j g x) -> p g j x", j=TPC, g=NG)
                    for tap in range(TAPS):
                        dst = taps[tap][:, blk, :, NB * tap:].rearrange("p g (j x) -> p g j x", j=TPC)
                        ins = nc.scalar.activation(dst, src, ACT.Copy, scale=wc[:, blk, TAPS - 1 - tap:TAPS - tap])
                ins.then_inc(bank_free[bank], 1)

            def silu_tile(p, f, c):
                act.wait_ge(conv_done, 2 * f + 2)
                if c is not None:
                    act.wait_ge(x3_done, 2 * f + p - 1)
                src = taps[0][:, :, :, p * TS * NB:(p + 1) * TS * NB].rearrange("p k g x -> p (k g) x")
                nc.scalar.activation(xct[p][:].rearrange("p k (g x) -> p (k g) x", g=NG), src, ACT.Silu).then_inc(silu_done, 1)

            def copy_xc(h, U, p, j, c):
                bank, before = bank_use(f"tr{h}.{j}", c)
                act.wait_ge(bank_ready[bank], before + 1)
                act.wait_ge(stacked, 64 * U)
                nc.scalar.activation(xn[p][:, h * HALF:(h + 1) * HALF], wb[bank][:], ACT.Copy)\
                    .then_inc(bank_free[bank], 1)

            def tanh_dt(U, j, c):
                act.wait_ge(*read_out(f"xp.{j}", c))
                act.wait_ge(x3_done, U)
                nc.scalar.activation(th[:], q48[:, 2 * DS:3 * DS], ACT.Tanh).then_inc(th_done, 1)

            def silu_gate(h, U, p, j, c):
                bank, before = bank_use(f"ga{h}.{j}", c)
                act.wait_ge(bank_ready[bank], before + 1)
                act.wait_ge(yg_done, U)
                nc.scalar.activation(sg[p][:, h * HALF:(h + 1) * HALF], wb[bank][:], ACT.Silu)\
                    .then_inc(bank_free[bank], 1)

            def square_and_high(U, p):
                act.wait_ge(xn_done, U + 1)
                act.wait_ge(nmin_done, U)
                nc.scalar.activation(sqj[:], xn[p][:], ACT.Square, accum_out=nsq[:]).then_inc(nsq_done, 1)
                act.wait_ge(stacked, 64 * U)
                nc.scalar.activation(xhi[:], xn[p][:], ACT.Copy).then_inc(hi_done, 1)

            def copy_yg(h, T, j, c):
                bank, before = bank_use(f"ot{h}.{j}", c)
                act.wait_ge(bank_ready[bank], before + 1)
                act.wait_ge(stored, 16 * T + STORED0)
                nc.scalar.activation(ygt[:, 4 * h:4 * h + 4, :], wb[bank][:].rearrange("p (k x) -> p k x", k=4), ACT.Copy)\
                    .then_inc(bank_free[bank], 1)

            act.wait_ge(loaded, 16 * LOADS)
            nc.scalar.activation(a2[:], a2[:], ACT.Tanh).then_inc(setup_a, 1)
            for q in range(4):
                scale_taps(q, 0, None)
            silu_tile(0, 0, None)
            silu_tile(1, 0, None)
            act.wait_ge(setup_v, SETUP_V)
            copy_xc(0, 0, 0, 1, None)
            copy_xc(1, 0, 0, 1, None)
            tanh_dt(0, 1, None)
            silu_gate(0, 0, 0, 1, None)
            square_and_high(0, 0)
            silu_gate(1, 0, 0, 1, None)
            with act.Fori(0, SETS) as s:
                with act.Fori(0, CPS) as k:
                    c = s * CPS + k
                    for j in range(TPC):
                        T = 2 * c + j
                        U = T + 1
                        copy_xc(0, U, 1 - j, j, c)
                        copy_xc(1, U, 1 - j, j, c)
                        if j == 0:
                            scale_taps(0, c + 1, c)
                        tanh_dt(U, j, c)
                        silu_gate(0, U, 1 - j, j, c)
                        if j == 0:
                            scale_taps(1, c + 1, c)
                        copy_yg(0, T, j, c)
                        copy_yg(1, T, j, c)
                        square_and_high(U, 1 - j)
                        if j == 0:
                            scale_taps(2, c + 1, c)
                            scale_taps(3, c + 1, c)
                            silu_tile(0, c + 1, c)
                        silu_gate(1, U, 1 - j, j, c)
                        if j == 0:
                            silu_tile(1, c + 1, c)
            copy_yg(0, TILES, 0, CHUNKS)
            copy_yg(1, TILES, 0, CHUNKS)

        @block.gpsimd
        def _(pool):
            def start_set(s, n):
                te = tembs[:, s, :, :]
                apart(pool)
                nc.gpsimd.tensor_tensor(cterm[:], te, wsum[:].unsqueeze(2).to_broadcast([P, KI, BSET]), ALU.mult)\
                    .then_inc(set_step, 1)
                pool.wait_ge(set_step, 8 * n + 1)
                nc.gpsimd.tensor_tensor(cterm[:], cterm[:], bc[:].unsqueeze(2).to_broadcast([P, KI, BSET]), ALU.add)\
                    .then_inc(set_step, 1)
                for tap in range(1, TAPS):
                    pool.wait_ge(set_step, 8 * n + 2 * tap)
                    apart(pool)
                    nc.gpsimd.tensor_tensor(halo[:], te, wneg[:, :, TAPS - 1 - tap:TAPS - tap].to_broadcast([P, KI, BSET]),
                                            ALU.mult).then_inc(set_step, 1)
                    pool.wait_ge(set_step, 8 * n + 2 * tap + 1)
                    apart(pool)
                    nc.gpsimd.tensor_copy(
                        taps[tap][:, :, :, 0:NB * tap].rearrange("p k g (t b) -> p (k g) t b", b=NB),
                        halo[:].rearrange("p k (g b) -> p (k g) b", g=NG).unsqueeze(2).to_broadcast([P, KI * NG, tap, NB]))\
                        .then_inc(set_step, 1)
                pool.wait_ge(set_step, 8 * n + 8)
                apart(pool)

            def convolve(hb, f, c):
                pool.wait_ge(*read_out(f"xr{2 * hb + 1}", c))
                if hb == 1:
                    pool.wait_ge(conv_done, 2 * f + 1)
                ks = slice(4 * hb, 4 * hb + 4)
                n = TPC * TS * NB
                acc = taps[0][:, ks, :, :].rearrange("p k g x -> p (k g) x")
                for tap in range(1, TAPS):
                    nc.gpsimd.tensor_tensor(acc, acc, taps[tap][:, ks, :, 0:n].rearrange("p k g x -> p (k g) x"), ALU.add)\
                        .then_inc(conv_step, 1)
                    pool.wait_ge(conv_step, (2 * f + hb) * 3 + tap)
                apart(pool)
                for tap in range(1, TAPS):
                    ins = nc.gpsimd.tensor_copy(taps[tap][:, ks, :, 0:NB * tap].rearrange("p k g x -> p (k g) x"),
                                                taps[tap][:, ks, :, n:n + NB * tap].rearrange("p k g x -> p (k g) x"))
                acc4 = taps[0][:, ks, :, :].rearrange("p k g (t b) -> p (k g) t b", b=NB)
                ct = cterm[:, ks, :].rearrange("p k (g b) -> p (k g) b", g=NG).unsqueeze(2)\
                    .to_broadcast([P, 4 * NG, TPC * TS, NB])
                nc.gpsimd.tensor_tensor(acc4, acc4, ct, ALU.add).then_inc(conv_done, 1)

            def inverse_std(U):
                pool.wait_ge(ve_done, U + 1)
                pool.wait_ge(x3_done, U)
                nc.gpsimd.tensor_tensor(rstd[:], ve[:], expo[:, 0:1], ALU.pow).then_inc(rstd_done, 1)

            def affine(U, p):
                pool.wait_ge(xhat_done, U + 1)
                nc.gpsimd.tensor_tensor(xn[p][:], xn[p][:], grow[:], ALU.mult).then_inc(aff_step, 1)
                pool.wait_ge(aff_step, U + 1)
                nc.gpsimd.tensor_tensor(xn[p][:], xn[p][:], brow[:], ALU.add).then_inc(xn_done, 1)

            def skip_term(U, p, j, c):
                pool.wait_ge(xn_done, U + 1)
                if c is not None:
                    pool.wait_ge(*read_out(f"ot1.{j}", c))
                nc.gpsimd.tensor_tensor(dx[p][:], xn[p][:], drow[:], ALU.mult).then_inc(dx_done, 1)

            def norm(U):
                pool.wait_ge(nsq_done, U + 1)
                pool.wait_ge(x3_done, U)
                apart(pool)
                nc.gpsimd.tensor_scalar(nmin[:], nsq[:], 1.0, 1.0, ALU.min, ALU.mult).then_inc(nmin_done, 1)
                pool.wait_ge(nmin_done, U + 1)
                nc.gpsimd.tensor_tensor(nrm[:], nmin[:], expo[:, 1:2], ALU.pow).then_inc(nrm_done, 1)

            def low_part(U, p):
                pool.wait_ge(hi_done, U + 1)
                pool.wait_ge(dx_done, U + 1)
                nc.gpsimd.tensor_tensor(xn[p][:], xn[p][:], xhi[:].bitcast(F32), ALU.subtract).then_inc(lo_done, 1)

            def apply_gate(T, p, j, c):
                pool.wait_ge(evac_done, T + 1)
                pool.wait_ge(*read_out(f"ga1.{j}", c, back=1))
                nc.gpsimd.tensor_tensor(dx[p][:], dx[p][:], sg[p][:], ALU.mult).then_inc(yg_done, 1)

            pool.wait_ge(loaded, 16 * LOADS)
            pool.wait_ge(setup_v, SETUP_V)
            start_set(0, 0)
            convolve(0, 0, None)
            convolve(1, 0, None)
            inverse_std(0)
            affine(0, 0)
            norm(0)
            skip_term(0, 0, 1, None)
            low_part(0, 0)
            with pool.Fori(0, SETS) as s:
                with pool.Fori(0, CPS) as k:
                    c = s * CPS + k
                    for j in range(TPC):
                        T = 2 * c + j
                        U = T + 1
                        if j == 0:
                            with pool.If(k == CPS - 1):
                                pool.wait_ge(conv_done, 2 * c + 2)
                                start_set(s + 1, s + 1)
                        inverse_std(U)
                        apply_gate(T, 1 - j, j, c)
                        affine(U, 1 - j)
                        norm(U)
                        skip_term(U, 1 - j, j, c)
                        low_part(U, 1 - j)
                        if j == 0:
                            convolve(0, c + 1, c)
                            convolve(1, c + 1, c)
            apply_gate(TILES, 1, 0, CHUNKS)

        @block.vector
        def _(dve):
            def statistics(U, p, j, c):
                if j == 1:
                    dve.wait_ge(*read_out("tr0.1", c))
                dve.wait_ge(*read_out(f"tr1.{j}", c))
                nc.vector.bn_stats(bst[:, 0, :], xn[p][:, 0:HALF])
                nc.vector.bn_stats(bst[:, 1, :], xn[p][:, HALF:DI]).then_inc(stat_step, 1)
                dve.wait_ge(stat_step, 2 * U + 1)
                apart(dve)
                nc.vector.bn_aggr(mv[:], bst[:].rearrange("p a b -> p (a b)")).then_inc(stat_step, 1)
                dve.wait_ge(stat_step, 2 * U + 2)
                dve.wait_ge(rstd_done, U)
                nc.vector.tensor_scalar(ve[:], mv[:, 1:2], EPS, None, ALU.add).then_inc(ve_done, 1)

            def normalise(U, p, j, c):
                bank, before = bank_use(f"xp.{j}", c)
                dve.wait_ge(rstd_done, U + 1)
                nc.vector.scalar_tensor_tensor(nmr[:], mv[:, 0:1], -1.0, rstd[:], ALU.mult, ALU.mult).then_inc(x3_step, 1)
                dve.wait_ge(x3_step, 4 * U + 1)
                nc.vector.tensor_scalar(xn[p][:], xn[p][:], rstd[:], nmr[:], ALU.mult, ALU.add).then_inc(xhat_done, 1)
                nc.vector.scalar_tensor_tensor(t48[:], s1[:], nmr[:], s2[:], ALU.mult, ALU.add).then_inc(x3_step, 1)
                dve.wait_ge(x3_step, 4 * U + 2)
                dve.wait_ge(bank_ready[bank], before + 1)
                dve.wait_ge(x3_done, U)
                nc.vector.scalar_tensor_tensor(q48[:], wb[bank][:, 0:NPROJ], rstd[:], t48[:], ALU.mult, ALU.add)\
                    .then_inc(bank_free[bank], 1)

            def expand(U, j, c):
                dve.wait_ge(*read_out(f"xp.{j}", c))
                dve.wait_ge(th_done, U + 1)
                dve.wait_ge(nrm_done, U + 1)
                dve.wait_ge(coef_done, U)
                nc.vector.tensor_tensor(ta[:], th[:], a2[:], ALU.mult).then_inc(x3_step, 1)
                m = msk[:].unsqueeze(2).to_broadcast([P, NB, DS])

                def wide(a):
                    return a.unsqueeze(1).to_broadcast([P, NB, DS])

                o = [x3[:, v, :].rearrange("p (b d) -> p b d", b=NB) for v in range(3)]
                nc.vector.scalar_tensor_tensor(o[0], wide(q48[:, 0:DS]), nrm[:], m, ALU.mult, ALU.mult)
                nc.vector.tensor_tensor(o[2], wide(q48[:, DS:2 * DS]), m, ALU.mult).then_inc(x3_step, 1)
                dve.wait_ge(x3_step, 4 * U + 4)
                nc.vector.scalar_tensor_tensor(o[1], wide(ta[:]), 1.0, m, ALU.add, ALU.mult).then_inc(x3_done, 1)

            def coefficients(U, p, j, c):
                bank, before = bank_use(f"sm.{j}", c)
                dve.wait_ge(bank_ready[bank], before + 1)
                dve.wait_ge(coef_done, U)
                n0 = 7 * U
                nc.vector.tensor_reduce(ba[:], wb[bank][:, 0:2 * P].rearrange("p (v n b) -> p v n b", v=2, b=NB),
                                        AX_X, ALU.add).then_inc(coef_step, 1)
                ad = ba[:, 1, :].rearrange("p (g t) -> p g t", g=NG)
                for t in range(TS):
                    dve.wait_ge(coef_step, n0 + t + 1)
                    prev = pcar[:] if t == 0 else pp[p][:, :, t - 1]
                    nc.vector.tensor_tensor(pp[p][:, :, t], prev, ad[:, :, t], ALU.mult).then_inc(coef_step, 1)
                dve.wait_ge(coef_step, n0 + 5)
                nc.vector.reciprocal(ip[:], pp[p][:].rearrange("p g t -> p (g t)")).then_inc(coef_step, 1)
                bank_c = wb[bank][:, 2 * P:3 * P].rearrange("p (g t b) -> p g t b", g=NG, t=TS)
                for t in range(TS):
                    ins = nc.vector.tensor_tensor(lhc[p][:, :, t, t * NB:(t + 1) * NB], bank_c[:, :, t, :],
                                                  pp[p][:, :, t:t + 1].to_broadcast([P, NG, NB]), ALU.mult)
                ins.then_inc(bank_free[bank], 1)
                dve.wait_ge(coef_step, n0 + 6)
                nc.vector.tensor_scalar(lim[p][:, 0, :], ip[:], CLIP, None, ALU.mult)
                nc.vector.tensor_scalar(lim[p][:, 1, :], ip[:], -CLIP, None, ALU.mult)
                nc.vector.tensor_tensor(bdp[p][:], ba[:, 0, :], ip[:], ALU.mult).then_inc(coef_step, 1)
                dve.wait_ge(coef_step, n0 + 7)
                nc.vector.tensor_copy(pcar[:], pp[p][:, :, TS - 1]).then_inc(coef_done, 1)

            def update(T, i, p):
                t, g = i // NG, i % NG
                col = g * TS + t
                dve.wait_ge(x_done, ITEMS * T + i + 1)
                if i == 0:
                    dve.wait_ge(coef_done, T + 1)
                if g == 0:
                    dve.wait_ge(y_done, TS * T + t - 1 + Y0)
                dve.wait_ge(clip_done, ITEMS * T + i + 1 + CLIP0 - 4)
                nc.vector.scalar_tensor_tensor(st[t % 2][:, g, :], px[i % 2][:], bdp[p][:, col:col + 1],
                                               st[1 - t % 2][:, g, :], ALU.mult, ALU.add).then_inc(upd_done, 1)

            def clip(T, i, p):
                t, g = i // NG, i % NG
                col = g * TS + t
                dve.wait_ge(upd_done, ITEMS * T + i + 1 + UPD0)
                nc.vector.tensor_scalar(st[t % 2][:, g, :], st[t % 2][:, g, :], lim[p][:, 0, col:col + 1],
                                        lim[p][:, 1, col:col + 1], ALU.min, ALU.max).then_inc(clip_done, 1)

            def read_y(T, p):
                dve.wait_ge(y_done, TS * T + Y0)
                dve.wait_ge(dx_done, T + 1)
                nc.vector.tensor_tensor(dx[p][:], py[:], dx[p][:], ALU.add).then_inc(evac_done, 1)

            def add_residual(T, j, c):
                bank, before = bank_use(f"ou.{j}", c)
                dve.wait_ge(bank_ready[bank], before + 1)
                dve.wait_ge(res_loaded, 16 * (T + 1))
                nc.vector.tensor_tensor(res[:], wb[bank][:], res[:], ALU.add)\
                    .then_inc(bank_free[bank], 1)

            dve.wait_ge(loaded, 16 * LOADS)
            nc.vector.memset(st[1][:, 0, 0:P], 1.0)
            nc.vector.tensor_copy(selr[:].rearrange("p a b -> p (a b)"), st[0][:, 0, :])
            nc.vector.tensor_copy(st[1][:, 1, :].rearrange("p (k x) -> p k x", k=KI), bcol[:].unsqueeze(2).to_broadcast([P, KI, P]))\
                .then_inc(setup_v, 1)
            dve.wait_ge(setup_t, 1)
            nc.vector.tensor_copy(wxg[:, :, 2 * DS:3 * DS], px[0][:, 0:KI * DS].rearrange("p (k x) -> p k x", k=KI))\
                .then_inc(setup_v, 1)
            dve.wait_ge(setup_v, 2)
            raw = st[1][:, 2, 0:KI * NPROJ].rearrange("p (k x) -> p k x", k=KI)
            nc.vector.tensor_copy(raw, wxg[:]).then_inc(setup_raw, 1)
            dve.wait_ge(setup_raw, 1)
            nc.vector.tensor_tensor(wxg[:], raw, gcol[:].unsqueeze(2).to_broadcast([P, KI, NPROJ]), ALU.mult).then_inc(setup_v, 1)
            dve.wait_ge(setup_t, 2)
            nc.vector.tensor_copy(s1[:], px[1][:, 0:NPROJ])
            nc.vector.tensor_tensor(s2[:], px[1][:, HALF:HALF + NPROJ], s2[:], ALU.add)
            dve.wait_ge(setup_a, 1)
            nc.vector.tensor_scalar(a2[:], a2[:], -0.01, None, ALU.mult)
            nc.vector.tensor_reduce(wsum[:], wc[:], AX_X, ALU.add)
            nc.vector.tensor_scalar(wneg[:], wc[:], -1.0, None, ALU.mult)
            nc.vector.memset(expo[:, 0:1], -0.5)
            nc.vector.memset(expo[:, 1:2], 0.5)
            nc.vector.memset(dx[1][:], 0.0)
            nc.vector.memset(sg[1][:], 0.0)
            nc.vector.memset(py[:], 0.0)
            nc.vector.memset(pcar[:], 1.0)
            nc.vector.memset(lhc[0][:], 0.0)
            nc.vector.memset(lhc[1][:], 0.0).then_inc(setup_v, 1)
            nc.vector.memset(st[0][:], 0.0).then_inc(upd_done, UPD0)
            nc.vector.memset(ve[:], 0.0).then_inc(clip_done, CLIP0)
            nc.vector.memset(nmr[:], 0.0).then_inc(y_done, Y0)
            dve.wait_ge(setup_v, SETUP_V)

            statistics(0, 0, 1, None)
            normalise(0, 0, 1, None)
            expand(0, 1, None)
            coefficients(0, 0, 1, None)
            with dve.Fori(0, SETS) as s:
                with dve.Fori(0, CPS) as k:
                    c = s * CPS + k
                    with dve.If(k == 0):
                        dve.wait_ge(y_done, 2 * TS * c + Y0)
                        nc.vector.memset(st[1][:], 0.0).then_inc(state_zero, 1)
                        dve.wait_ge(state_zero, s + 1)
                        apart(dve)
                    for j in range(TPC):
                        T = 2 * c + j
                        U = T + 1
                        for i in range(ITEMS):
                            if i == 2:
                                read_y(T, 1 - j)
                            if i == 4:
                                statistics(U, 1 - j, j, c)
                            if i == 6:
                                normalise(U, 1 - j, j, c)
                            if i == 11:
                                expand(U, j, c)
                            if i == 14:
                                add_residual(T, j, c)
                            if i == 15:
                                if j == 1:
                                    with dve.If(k == CPS - 1):
                                        dve.wait_ge(coef_done, U)
                                        nc.vector.memset(pcar[:], 1.0).then_inc(decay_reset, 1)
                                        dve.wait_ge(decay_reset, s + 1)
                                        apart(dve)
                                coefficients(U, 1 - j, j, c)
                            update(T, i, j)
                            if i >= 1:
                                clip(T, i - 1, j)
                        clip(T, ITEMS - 1, j)
            read_y(TILES, 1)
            add_residual(TILES, 0, CHUNKS)


SETUP_V = 4


def kernel(x, cond_2048, L0_cond_W_in, L0_cond_W_conv, L0_cond_b_conv, L0_cond_ln_g, L0_cond_ln_b, L0_cond_W_xproj,
           L0_cond_W_dt, L0_cond_b_dt, L0_cond_A_log, L0_cond_D, L0_cond_W_out):
    import numpy as np
    import concourse.bacc as bacc
    from concourse.bass_utils import run_bass_kernel_spmd

    def cols(v):
        return np.ascontiguousarray(np.asarray(v).reshape(KI, P).T)

    def rows(v, n=P):
        return np.ascontiguousarray(np.broadcast_to(np.asarray(v), (n, np.asarray(v).shape[0])))

    x = np.asarray(x)
    tiles = x.reshape(SETS, NG, NB, CPS, TPC, TS, DM).transpose(0, 3, 4, 1, 5, 2, 6).reshape(TILES, P, DM)
    xT = np.zeros((CHUNKS + 1, P, KD, CH), np.float32)
    xT[:CHUNKS] = tiles.reshape(CHUNKS, CH, KD, P).transpose(0, 3, 2, 1)
    xtok = np.zeros((TILES + 1, P, DM), np.float32)
    xtok[1:] = tiles
    temb = np.zeros((P, SETS + 1, KI, BSET), np.float32)
    temb[:, :SETS] = np.asarray(cond_2048).reshape(SETS, BSET, KI, P).transpose(3, 0, 2, 1)
    w_x = np.asarray(L0_cond_W_xproj)
    b_dt = np.zeros((P, NPROJ), np.float32)
    b_dt[:, 2 * DS:] = np.asarray(L0_cond_b_dt)
    row = np.arange(P)
    sel = np.zeros((P, 2 * TS, NB, DS), np.float32)
    sel[row, (row % 64) // NB, row % NB, :] = 1.0
    mask = np.zeros((P, NB), np.float32)
    mask[row, row % NB] = 1.0
    arrays = {
        "xT": xT, "xtok": xtok, "temb": temb,
        "w_in": np.ascontiguousarray(np.asarray(L0_cond_W_in).T.reshape(KD, P, 2 * DI).transpose(1, 0, 2)),
        "w_conv": np.ascontiguousarray(np.asarray(L0_cond_W_conv).reshape(KI, P, TAPS).transpose(1, 0, 2)),
        "b_conv": cols(L0_cond_b_conv), "ln_g": cols(L0_cond_ln_g), "ln_b": cols(L0_cond_ln_b),
        "g_rows": rows(L0_cond_ln_g), "b_rows": rows(L0_cond_ln_b), "d_rows": rows(L0_cond_D),
        "w_x": np.ascontiguousarray(w_x.T.reshape(KI, P, NPROJ).transpose(1, 0, 2)),
        "w_x3": np.ascontiguousarray(w_x[2 * DS:]),
        "w_dt": np.ascontiguousarray(np.asarray(L0_cond_W_dt).T),
        "b_dt": b_dt, "a_log": rows(L0_cond_A_log),
        "w_out": np.ascontiguousarray(np.asarray(L0_cond_W_out).T.reshape(KI, P, DM).transpose(1, 0, 2)),
        "ident": np.eye(P, dtype=np.float32), "sel": sel.reshape(P, 2 * TS, P), "mask": mask,
    }
    nc = bacc.Bacc("TRN2", target_bir_lowering=False, num_devices=1, dynamic_dma_scratch_size=1024)
    aps = [nc.dram_tensor(f"in_{n}", a.shape, mybir.dt.from_np(a.dtype), kind="ExternalInput").ap() for n, a in arrays.items()]
    order = dict(zip(arrays, aps))
    result = nc.dram_tensor("out", (TILES + 1, P, DM), F32, kind="ExternalOutput").ap()
    build(nc, out=result, **order)
    r = run_bass_kernel_spmd(nc, [{f"in_{n}": a for n, a in arrays.items()}], core_ids=[0])
    got = r.results[0]["out"]
    return np.ascontiguousarray(
        got[1:].reshape(SETS, CPS, TPC, NG, TS, NB, DM).transpose(0, 3, 5, 1, 2, 4, 6).reshape(BATCH, SEQ, DM))
```

```python
from contextlib import ExitStack

import concourse.bass as bass
from concourse import mybir

F32 = mybir.dt.float32
F32R = mybir.dt.float32r
BF16 = mybir.dt.bfloat16
ALU = mybir.AluOpType
ACT = mybir.ActivationFunctionType
AX_X = mybir.AxisListType.X

P = 128
BATCH, SEQ, DM, DI, DS = 128, 128, 512, 1024, 16
NB, TS, NG = 8, 4, 4
BSET = NG * NB
SETS = BATCH // BSET
TPC = 2
CH = TPC * P
CPS = SEQ // (TS * TPC)
CHUNKS = SETS * CPS
TILES = CHUNKS * TPC
KD = DM // P
KI = DI // P
HALF = 512
ITEMS = TS * NG
TAPS = 4
CLIP = 10.0
EPS = 1e-5
NPROJ = 3 * DS
PROJ = 64

HALVES = {
    0: ["tr0", "tr1", "xp", "ga1", "xrB", "sm"],
    1: ["ga0", "xrA", "xq", "ot0", "ot1", "ou"],
}
BODY = {b: [f"{u}.{j}" for j in range(TPC) for u in HALVES[b]] for b in HALVES}
BEFORE = {0: ["first0", "first2"] + BODY[0][6:], 1: ["first1", "first3", "ga0.1", "xrA.1", "xq.1"]}
AFTER = {0: [], 1: ["ot0.0", "ot1.0", "ou.0"]}


def bank_use(name, c, back=0):
    last = isinstance(c, int) and c == CHUNKS and back == 0
    for bank in (0, 1):
        order = BEFORE[bank] if c is None else AFTER[bank] if last else BODY[bank]
        if name in order:
            if c is None:
                return bank, order.index(name)
            return bank, c * len(BODY[bank]) + (len(BEFORE[bank]) + order.index(name) - back * len(BODY[bank]))
    raise KeyError(name)


def build(nc, xT, xtok, temb, w_in, w_conv, b_conv, ln_g, ln_b, g_rows, b_rows, d_rows, w_x, w_x3,
          w_dt, b_dt, a_log, w_out, ident, sel, mask, out):
    with ExitStack() as ctx:
        def sb(name, shape, dt=F32):
            return ctx.enter_context(nc.sbuf_tensor(name, shape, dt))

        def psum(name, shape):
            return ctx.enter_context(nc.psum_tensor(name, shape, F32))

        def sem(name):
            return ctx.enter_context(nc.semaphore(name))

        win = sb("win", [P, KD, 2 * DI])
        wout = sb("wout", [P, KI, DM])
        wxg = sb("wxg", [P, KI, PROJ])
        wc = sb("wc", [P, KI, TAPS])
        wneg = sb("wneg", [P, KI, TAPS])
        wsum = sb("wsum", [P, KI])
        bc = sb("bc", [P, KI])
        gcol = sb("gcol", [P, KI])
        bcol = sb("bcol", [P, KI])
        grow = sb("grow", [P, DI])
        brow = sb("brow", [P, DI])
        drow = sb("drow", [P, DI])
        tembs = sb("tembs", [P, SETS + 1, KI, BSET])
        idn = sb("idn", [P, P])
        selr = sb("selr", [P, 8, P], F32R)
        msk = sb("msk", [P, NB])
        s1 = sb("s1", [P, NPROJ])
        s2 = sb("s2", [P, NPROJ])
        a2 = sb("a2", [P, DS])
        expo = sb("expo", [P, 2])
        wdt = sb("wdt", [DS, DS])
        xt = sb("xt", [P, KD, CH])
        xg = sb("xg", [P, KD, CH])
        taps = [sb(f"taps{s}", [P, KI, NG, NB * (s + TS * TPC)]) for s in range(TAPS)]
        cterm = sb("cterm", [P, KI, BSET])
        halo = [None] + [sb(f"halo{s}", [P, KI, BSET]) for s in range(1, TAPS)]
        xct = [sb(f"xct{p}", [P, KI, P]) for p in range(2)]
        xn = [sb(f"xn{p}", [P, DI]) for p in range(2)]
        xhi = sb("xhi", [P, DI], F32R)
        sqj = sb("sqj", [P, DI], BF16)
        stack = [sb(f"stack{p}", [P, 2, DI], F32R) for p in range(2)]
        dx = [sb(f"dx{p}", [P, DI]) for p in range(2)]
        sg = [sb(f"sg{p}", [P, DI]) for p in range(2)]
        bst = sb("bst", [P, 2, 6])
        mv = sb("mv", [P, 2])
        ve = sb("ve", [P, 1])
        rstd = sb("rstd", [P, 1])
        nmr = sb("nmr", [P, 1])
        t48 = sb("t48", [P, NPROJ])
        q48 = sb("q48", [P, NPROJ])
        pq = sb("pq", [P, P])
        th = sb("th", [P, DS])
        ta = sb("ta", [P, DS])
        nsq = sb("nsq", [P, 1])
        nmin = sb("nmin", [P, 1])
        nrm = sb("nrm", [P, 1])
        x3 = sb("x3", [P, 3, P])
        ba = sb("ba", [P, 2, ITEMS])
        pcar = sb("pcar", [P, NG])
        pp = [sb(f"pp{p}", [P, NG, TS]) for p in range(2)]
        ip = sb("ip", [P, ITEMS])
        lim = [sb(f"lim{p}", [P, 2, ITEMS]) for p in range(2)]
        bdp = [sb(f"bdp{p}", [P, ITEMS]) for p in range(2)]
        lhc = [sb(f"lhc{p}", [P, NG, TS, BSET]) for p in range(2)]
        st = [sb(f"st{p}", [P, NG, DI]) for p in range(2)]
        wx3 = st[1][0:DS, 3, :]
        ygt = sb("ygt", [P, KI, P])
        res = sb("res", [P, DM])

        px = [psum(f"px{p}", [P, DI]) for p in range(2)]
        py = psum("py", [P, DI])
        wb = [psum(f"wb{p}", [P, HALF]) for p in range(2)]

        loaded = sem("loaded")
        setup_v = sem("setup_v")
        setup_t = sem("setup_t")
        setup_a = sem("setup_a")
        setup_raw = sem("setup_raw")
        xt_loaded = sem("xt_loaded")
        xg_loaded = sem("xg_loaded")
        bank_ready = [sem(f"bank_ready{p}") for p in range(2)]
        bank_free = [sem(f"bank_free{p}") for p in range(2)]
        conv_step = sem("conv_step")
        conv_done = sem("conv_done")
        halo_moved = sem("halo_moved")
        set_step = sem("set_step")
        set_ready = sem("set_ready")
        silu_done = sem("silu_done")
        stat_step = sem("stat_step")
        ve_done = sem("ve_done")
        rstd_done = sem("rstd_done")
        xhat_done = sem("xhat_done")
        q_done = sem("q_done")
        aff_step = sem("aff_step")
        xn_done = sem("xn_done")
        th_done = sem("th_done")
        nsq_done = sem("nsq_done")
        nmin_done = sem("nmin_done")
        nrm_done = sem("nrm_done")
        hi_done = sem("hi_done")
        dx_done = sem("dx_done")
        lo_done = sem("lo_done")
        stacked = sem("stacked")
        x3_step = sem("x3_step")
        x3_done = sem("x3_done")
        coef_step = sem("coef_step")
        coef_done = sem("coef_done")
        x_done = sem("x_done")
        upd_done = sem("upd_done")
        clip_done = sem("clip_done")
        y_done = sem("y_done")
        state_zero = sem("state_zero")
        decay_reset = sem("decay_reset")
        evac_done = sem("evac_done")
        yg_done = sem("yg_done")
        res_loaded = sem("res_loaded")
        stored = sem("stored")

        UPD0 = 2
        CLIP0 = 4
        Y0 = 2
        STORED0 = 16

        def apart(eng):
            eng.nop(nofuse=True)

        def vacant(name, c):
            bank, before = bank_use(name, c)
            return bank_free[bank], before

        def filled(name, c):
            bank, before = bank_use(name, c)
            return bank_ready[bank], before + 1

        def read_out(name, c, back=0):
            bank, before = bank_use(name, c, back)
            return bank_free[bank], before + 1

        LOADS = 18

        block = ctx.enter_context(nc.Block())

        @block.sync
        def _(sp):
            for dst, src in ((idn, ident), (wx3, w_x3), (wdt, w_dt), (wc, w_conv), (bc, b_conv), (gcol, ln_g),
                             (bcol, ln_b), (wxg[:, :, 0:NPROJ], w_x), (s2, b_dt), (a2, a_log), (msk, mask), (tembs, temb),
                             (win, w_in), (wout, w_out), (grow, g_rows), (brow, b_rows), (drow, d_rows),
                             (st[0][:, 0, :].rearrange("p (a b) -> p a b", a=8), sel)):
                sp.dma_start(dst[:], src).then_inc(loaded, 16)

            def load_chunk(f, c):
                if c is not None:
                    sp.wait_ge(*read_out("xrB.0", c))
                sp.wait_ge(xg_loaded, 16 * f)
                sp.dma_start(xt[:], xT[f]).then_inc(xt_loaded, 16)

            def keep_for_gates(f, c):
                sp.wait_ge(xt_loaded, 16 * f + 16)
                if c is not None:
                    sp.wait_ge(*read_out("ga1.0", c))
                sp.dma_start(xg[:], xt[:]).then_inc(xg_loaded, 16)

            def stack_parts(U, p, c):
                sp.wait_ge(hi_done, U + 1)
                apart(sp)
                sp.wait_ge(lo_done, U + 1)
                apart(sp)
                if p == 1 or c is not None:
                    sp.wait_ge(x_done, ITEMS * (U - 1) + 1)
                hi, lo, st32 = xhi[:].bitcast(F32), xn[p], stack[p][:].bitcast(F32)
                for pair in range(2):
                    rows = slice(64 * pair, 64 * pair + 64)
                    sp.dma_start(st32[0:64, pair, :], hi[rows, :]).then_inc(stacked, 16)
                    sp.dma_start(st32[64:128, pair, :], lo[rows, :]).then_inc(stacked, 16)

            def load_residual(T):
                sp.wait_ge(stored, 16 * T + STORED0)
                sp.dma_start(res[:], xtok[T]).then_inc(res_loaded, 16)

            def store(T, j, c):
                sp.wait_ge(*read_out(f"ou.{j}", c))
                sp.dma_start(out[T], res[:]).then_inc(stored, 16)

            sp.sem_inc(stored, STORED0)
            load_chunk(0, None)
            keep_for_gates(0, None)
            sp.wait_ge(*read_out("first3", None))
            load_chunk(1, None)
            stack_parts(0, 0, None)
            with sp.Fori(0, SETS) as s:
                with sp.Fori(0, CPS) as k:
                    c = s * CPS + k
                    load_residual(2 * c)
                    keep_for_gates(c + 1, c)
                    load_chunk(c + 2, c)
                    stack_parts(2 * c + 1, 1, c)
                    store(2 * c, 0, c)
                    load_residual(2 * c + 1)
                    stack_parts(2 * c + 2, 0, c)
                    store(2 * c + 1, 1, c)
            load_residual(TILES)
            store(TILES, 0, CHUNKS)
            sp.wait_ge(stored, 16 * (TILES + 1) + STORED0)

        @block.tensor
        def _(pe):
            def input_blocks(name, q, part, f, c):
                bank, _ = bank_use(name, c)
                if part == 0:
                    pe.wait_ge(*vacant(name, c))
                    if q in (0, 2):
                        pe.wait_ge(xt_loaded, 16 * f + 16)
                blk = 2 * q + part
                for kd in range(KD):
                    mm = nc.tensor.matmul(wb[bank][:, part * CH:(part + 1) * CH], win[:, kd, blk * P:(blk + 1) * P],
                                          xt[:, kd, :], start=(kd == 0), stop=(kd == KD - 1))
                if part == 1:
                    mm.then_inc(bank_ready[bank], 1)

            def turn_xc(h, U, p, j, c):
                bank, _ = bank_use(f"tr{h}.{j}", c)
                ps = wb[bank]
                pe.wait_ge(*vacant(f"tr{h}.{j}", c))
                pe.wait_ge(silu_done, U + 1)
                for b in range(4):
                    mm = nc.tensor.transpose(ps[:, b * P:(b + 1) * P], xct[p][:, 4 * h + b, :], idn[:])
                mm.then_inc(bank_ready[bank], 1)

            def project_bcd(U, p, j, c):
                bank, _ = bank_use(f"xp.{j}", c)
                pe.wait_ge(*vacant(f"xp.{j}", c))
                for b in range(4):
                    for h in range(2):
                        mm = nc.tensor.matmul(wb[bank][PROJ * h:PROJ * (h + 1), 0:P], wxg[:, 4 * h + b, :],
                                              xct[p][:, 4 * h + b, :], start=(b == 0), stop=(b == 3),
                                              tile_position=(0, PROJ * h))
                mm.then_inc(bank_ready[bank], 1)

            def turn_bcd(U, j, c):
                bank, _ = bank_use(f"xq.{j}", c)
                pe.wait_ge(*vacant(f"xq.{j}", c))
                pe.wait_ge(*read_out(f"xp.{j}", c))
                nc.tensor.transpose(wb[bank][:, 0:P], pq[:], idn[:]).then_inc(bank_ready[bank], 1)

            def gate(h, part, U, p, j, c):
                if part == 0:
                    pe.wait_ge(*vacant(f"ga{h}.{j}", c))
                    pe.wait_ge(xg_loaded, 16 * (c + 1 + j) if c is not None else 16)
                bank, _ = bank_use(f"ga{h}.{j}", c)
                src = xg[:, :, (1 - j) * P:(2 - j) * P]
                for kd in (2 * part, 2 * part + 1):
                    mm = nc.tensor.matmul(wb[bank][:], src[:, kd, :],
                                          win[:, kd, DI + h * HALF:DI + (h + 1) * HALF], start=(kd == 0), stop=(kd == KD - 1))
                if part == 1:
                    mm.then_inc(bank_ready[bank], 1)

            def turn_coefs(U, j, c):
                bank, _ = bank_use(f"sm.{j}", c)
                ps = wb[bank]
                pe.wait_ge(*vacant(f"sm.{j}", c))
                pe.wait_ge(x3_done, U + 1)
                for v in range(3):
                    mm = nc.tensor.transpose(ps[:, v * P:(v + 1) * P], x3[:, v, :], idn[:])
                mm.then_inc(bank_ready[bank], 1)

            def spread(T, i, p):
                if i == 0:
                    pe.wait_ge(stacked, 64 * (T + 1))
                t, g = i // NG, i % NG
                pe.wait_ge(upd_done, ITEMS * T + i + 1 + UPD0 - 2)
                for h in range(2):
                    mm = nc.tensor.matmul(px[i % 2][:, h * HALF:(h + 1) * HALF], selr[:, (g % 2) * TS + t, :],
                                          stack[p][:, g // 2, h * HALF:(h + 1) * HALF], start=True, stop=True)
                mm.then_inc(x_done, 1)

            def contract(T, t, p):
                if t == 0:
                    pe.wait_ge(coef_done, T + 1)
                    pe.wait_ge(evac_done, T + 1)
                pe.wait_ge(clip_done, ITEMS * T + NG * t + NG + CLIP0)
                for h in range(2):
                    for g in range(NG):
                        mm = nc.tensor.matmul(py[g * BSET:(g + 1) * BSET, h * HALF:(h + 1) * HALF], lhc[p][:, g, t, :],
                                              st[t % 2][:, g, h * HALF:(h + 1) * HALF],
                                              start=(t == 0), stop=(t == TS - 1), tile_position=(0, g * BSET))
                mm.then_inc(y_done, 1)

            def turn_yg(h, T, j, c):
                bank, _ = bank_use(f"ot{h}.{j}", c)
                ps = wb[bank]
                pe.wait_ge(*vacant(f"ot{h}.{j}", c))
                pe.wait_ge(yg_done, T + 1)
                for b in range(4):
                    mm = nc.tensor.transpose(ps[:, b * P:(b + 1) * P], dx[1 - j][:, (4 * h + b) * P:(4 * h + b + 1) * P], idn[:])
                mm.then_inc(bank_ready[bank], 1)

            def project_out(part, T, j, c):
                if part == 0:
                    pe.wait_ge(*vacant(f"ou.{j}", c))
                bank, _ = bank_use(f"ou.{j}", c)
                for blk in (2 * part, 2 * part + 1):
                    mm = nc.tensor.matmul(wb[bank][:], ygt[:, blk, :], wout[:, blk, :], start=(blk == 0), stop=(blk == KI - 1))
                if part == 3:
                    mm.then_inc(bank_ready[bank], 1)

            pe.wait_ge(loaded, 16 * LOADS)
            for blk in range(KI):
                mm = nc.tensor.matmul(px[0][:, blk * DS:(blk + 1) * DS], wx3[:, blk * P:(blk + 1) * P], wdt[:],
                                      start=True, stop=True)
            mm.then_inc(setup_t, 1)
            pe.wait_ge(setup_v, 3)
            for blk in range(KI):
                nc.tensor.matmul(px[1][:, 0:NPROJ], st[1][:, 0, 0:P], wxg[:, blk, 0:NPROJ], start=(blk == 0), stop=(blk == KI - 1))
            for blk in range(KI):
                mm = nc.tensor.matmul(px[1][:, HALF:HALF + NPROJ], st[1][:, 1, blk * P:(blk + 1) * P],
                                      st[1][:, 2, blk * NPROJ:(blk + 1) * NPROJ], start=(blk == 0), stop=(blk == KI - 1))
            mm.then_inc(setup_t, 1)

            def front(n, U, p, j, c):
                if n in (0, 1):
                    turn_xc(n, U, p, j, c)
                    gate(0, n, U, p, j, c)
                if n == 2:
                    project_bcd(U, p, j, c)
                if n in (5, 6):
                    gate(1, n - 5, U, p, j, c)
                if n == 6:
                    turn_bcd(U, j, c)
                if n == 12:
                    turn_coefs(U, j, c)

            def convs(n, f, j, c):
                if n in (2, 4):
                    input_blocks(f"xrA.{j}", 2 - 2 * j, n // 2 - 1, f, c)
                if n in (8, 9):
                    input_blocks(f"xrB.{j}", 3 - 2 * j, n - 8, f, c)

            for q in range(4):
                for part in range(2):
                    input_blocks(f"first{q}", q, part, 0, None)
            pe.wait_ge(setup_v, SETUP_V)
            for n in range(ITEMS):
                front(n, 0, 0, 1, None)
                convs(n, 1, 1, None)
            spread(0, 0, 0)
            spread(0, 1, 0)
            with pe.Fori(0, SETS) as s:
                with pe.Fori(0, CPS) as k:
                    c = s * CPS + k
                    for j in range(TPC):
                        T = 2 * c + j
                        for n in range(ITEMS):
                            if n + 2 < ITEMS:
                                spread(T, n + 2, j)
                            else:
                                spread(T + 1, n + 2 - ITEMS, 1 - j)
                            front(n, T + 1, 1 - j, j, c)
                            if n in (8, 9):
                                turn_yg(n - 8, T, j, c)
                            convs(n, c + 1 + j, j, c)
                            if n in (10, 12, 13, 14):
                                project_out((10, 12, 13, 14).index(n), T, j, c)
                            if n % NG == NG - 1:
                                contract(T, n // NG, j)
            for h in range(2):
                turn_yg(h, TILES, 0, CHUNKS)
            for part in range(4):
                project_out(part, TILES, 0, CHUNKS)

        @block.scalar
        def _(act):
            def move_halo(q):
                n = TPC * TS * NB
                for tap in range(1, TAPS):
                    arr = taps[tap][:, 2 * q:2 * q + 2, :, :].rearrange("p k g x -> p (k g) x")
                    ins = nc.scalar.activation(arr[:, :, 0:NB * tap], arr[:, :, n:n + NB * tap], ACT.Copy)
                ins.then_inc(halo_moved, 1)

            def start_halo(q):
                for tap in range(1, TAPS):
                    for t in range(tap):
                        ins = nc.scalar.activation(
                            taps[tap][:, 2 * q:2 * q + 2, :, NB * t:NB * (t + 1)].rearrange("p k g b -> p (k g) b"),
                            halo[tap][:, 2 * q:2 * q + 2, :].rearrange("p k (g b) -> p (k g) b", g=NG), ACT.Copy)
                ins.then_inc(halo_moved, 1)

            def scale_taps(name, q, f, c):
                bank, _ = bank_use(name, c)
                act.wait_ge(*filled(name, c))
                act.wait_ge(halo_moved, 4 * f + q + 1)
                for part in range(2):
                    blk = 2 * q + part
                    src = wb[bank][:, part * CH:(part + 1) * CH].rearrange("p (j g x) -> p g j x", j=TPC, g=NG)
                    for tap in range(TAPS):
                        dst = taps[tap][:, blk, :, NB * tap:].rearrange("p g (j x) -> p g j x", j=TPC)
                        ins = nc.scalar.activation(dst, src, ACT.Copy, scale=wc[:, blk, TAPS - 1 - tap:TAPS - tap])
                ins.then_inc(bank_free[bank], 1)

            def silu_tile(p, f, c):
                act.wait_ge(conv_done, 4 * f + 4)
                if c is not None:
                    act.wait_ge(x3_done, 2 * f + p - 1)
                src = taps[0][:, :, :, p * TS * NB:(p + 1) * TS * NB].rearrange("p k g x -> p (k g) x")
                nc.scalar.activation(xct[p][:].rearrange("p k (g x) -> p (k g) x", g=NG), src, ACT.Silu).then_inc(silu_done, 1)

            def copy_xc(h, U, p, j, c):
                bank, before = bank_use(f"tr{h}.{j}", c)
                act.wait_ge(bank_ready[bank], before + 1)
                act.wait_ge(stacked, 64 * U)
                nc.scalar.activation(xn[p][:, h * HALF:(h + 1) * HALF], wb[bank][:], ACT.Copy)\
                    .then_inc(bank_free[bank], 1)

            def copy_bcd(U, j, c):
                bank, before = bank_use(f"xp.{j}", c)
                act.wait_ge(*filled(f"xp.{j}", c))
                act.wait_ge(x3_done, U)
                nc.scalar.activation(pq[:], wb[bank][:, 0:P], ACT.Copy).then_inc(bank_free[bank], 1)

            def tanh_dt(U, j, c):
                act.wait_ge(q_done, U + 1)
                act.wait_ge(x3_done, U)
                nc.scalar.activation(th[:], q48[:, 2 * DS:3 * DS], ACT.Tanh).then_inc(th_done, 1)

            def silu_gate(h, U, p, j, c):
                bank, before = bank_use(f"ga{h}.{j}", c)
                act.wait_ge(bank_ready[bank], before + 1)
                act.wait_ge(yg_done, U)
                nc.scalar.activation(sg[p][:, h * HALF:(h + 1) * HALF], wb[bank][:], ACT.Silu)\
                    .then_inc(bank_free[bank], 1)

            def square_and_high(U, p):
                act.wait_ge(xn_done, U + 1)
                act.wait_ge(nmin_done, U)
                nc.scalar.activation(sqj[:], xn[p][:], ACT.Square, accum_out=nsq[:]).then_inc(nsq_done, 1)
                act.wait_ge(stacked, 64 * U)
                nc.scalar.activation(xhi[:], xn[p][:], ACT.Copy).then_inc(hi_done, 1)

            def copy_yg(h, T, j, c):
                bank, before = bank_use(f"ot{h}.{j}", c)
                act.wait_ge(bank_ready[bank], before + 1)
                act.wait_ge(stored, 16 * T + STORED0)
                nc.scalar.activation(ygt[:, 4 * h:4 * h + 4, :], wb[bank][:].rearrange("p (k x) -> p k x", k=4), ACT.Copy)\
                    .then_inc(bank_free[bank], 1)

            act.wait_ge(loaded, 16 * LOADS)
            nc.scalar.activation(a2[:], a2[:], ACT.Tanh).then_inc(setup_a, 1)
            act.wait_ge(set_ready, 1)
            for q in range(4):
                start_halo(q)
                scale_taps(f"first{q}", q, 0, None)
            silu_tile(0, 0, None)
            silu_tile(1, 0, None)
            act.wait_ge(setup_v, SETUP_V)
            copy_xc(0, 0, 0, 1, None)
            copy_xc(1, 0, 0, 1, None)
            silu_gate(0, 0, 0, 1, None)
            copy_bcd(0, 1, None)
            act.wait_ge(conv_done, 4 + 0 - 3)
            move_halo(0)
            scale_taps("xrA.1", 0, 1, None)
            silu_gate(1, 0, 0, 1, None)
            tanh_dt(0, 1, None)
            square_and_high(0, 0)
            act.wait_ge(conv_done, 4 + 1 - 3)
            move_halo(1)
            scale_taps("xrB.1", 1, 1, None)
            with act.Fori(0, SETS) as s:
                with act.Fori(0, CPS) as k:
                    c = s * CPS + k
                    for j in range(TPC):
                        T = 2 * c + j
                        U = T + 1
                        f = c + 1 + j
                        q = 2 - 2 * j
                        copy_xc(0, U, 1 - j, j, c)
                        copy_xc(1, U, 1 - j, j, c)
                        silu_gate(0, U, 1 - j, j, c)
                        copy_bcd(U, j, c)
                        act.wait_ge(conv_done, 4 * f + q - 3)
                        apart(act)
                        with act.If(k == CPS - 1 - j):
                            act.wait_ge(set_ready, s + 2)
                            start_halo(q)
                        with act.Else():
                            move_halo(q)
                        scale_taps(f"xrA.{j}", q, f, c)
                        silu_gate(1, U, 1 - j, j, c)
                        tanh_dt(U, j, c)
                        square_and_high(U, 1 - j)
                        copy_yg(0, T, j, c)
                        copy_yg(1, T, j, c)
                        act.wait_ge(conv_done, 4 * f + q - 2)
                        apart(act)
                        with act.If(k == CPS - 1 - j):
                            start_halo(q + 1)
                        with act.Else():
                            move_halo(q + 1)
                        scale_taps(f"xrB.{j}", q + 1, f, c)
                        if j == 0:
                            silu_tile(0, f, c)
                            silu_tile(1, f, c)
            copy_yg(0, TILES, 0, CHUNKS)
            copy_yg(1, TILES, 0, CHUNKS)

        @block.gpsimd
        def _(pool):
            def start_set(s, n):
                te = tembs[:, s, :, :]
                apart(pool)
                nc.gpsimd.tensor_tensor(cterm[:], te, wsum[:].unsqueeze(2).to_broadcast([P, KI, BSET]), ALU.mult)\
                    .then_inc(set_step, 1)
                pool.wait_ge(set_step, 2 * n + 1)
                nc.gpsimd.tensor_tensor(cterm[:], cterm[:], bc[:].unsqueeze(2).to_broadcast([P, KI, BSET]), ALU.add)\
                    .then_inc(set_step, 1)
                for tap in range(1, TAPS):
                    ins = nc.gpsimd.tensor_tensor(halo[tap][:], te, wneg[:, :, TAPS - 1 - tap:TAPS - tap].to_broadcast([P, KI, BSET]),
                                                  ALU.mult)
                ins.then_inc(set_ready, 1)

            def convolve(name, q, f, c):
                pool.wait_ge(*read_out(name, c))
                ks = slice(2 * q, 2 * q + 2)
                n = TPC * TS * NB
                acc = taps[0][:, ks, :, :].rearrange("p k g x -> p (k g) x")
                for tap in range(1, TAPS):
                    nc.gpsimd.tensor_tensor(acc, acc, taps[tap][:, ks, :, 0:n].rearrange("p k g x -> p (k g) x"), ALU.add)\
                        .then_inc(conv_step, 1)
                    pool.wait_ge(conv_step, (4 * f + q) * 3 + tap)
                acc4 = taps[0][:, ks, :, :].rearrange("p k g (t b) -> p (k g) t b", b=NB)
                ct = cterm[:, ks, :].rearrange("p k (g b) -> p (k g) b", g=NG).unsqueeze(2)\
                    .to_broadcast([P, 2 * NG, TPC * TS, NB])
                nc.gpsimd.tensor_tensor(acc4, acc4, ct, ALU.add).then_inc(conv_done, 1)

            def inverse_std(U):
                pool.wait_ge(ve_done, U + 1)
                pool.wait_ge(x3_done, U)
                nc.gpsimd.tensor_tensor(rstd[:], ve[:], expo[:, 0:1], ALU.pow).then_inc(rstd_done, 1)

            def affine(U, p):
                pool.wait_ge(xhat_done, U + 1)
                nc.gpsimd.tensor_tensor(xn[p][:], xn[p][:], grow[:], ALU.mult).then_inc(aff_step, 1)
                pool.wait_ge(aff_step, U + 1)
                nc.gpsimd.tensor_tensor(xn[p][:], xn[p][:], brow[:], ALU.add).then_inc(xn_done, 1)

            def skip_term(U, p, j, c):
                pool.wait_ge(xn_done, U + 1)
                if c is not None:
                    pool.wait_ge(*read_out(f"ot1.{j}", c))
                nc.gpsimd.tensor_tensor(dx[p][:], xn[p][:], drow[:], ALU.mult).then_inc(dx_done, 1)

            def norm(U):
                pool.wait_ge(nsq_done, U + 1)
                pool.wait_ge(x3_done, U)
                apart(pool)
                nc.gpsimd.tensor_scalar(nmin[:], nsq[:], 1.0, 1.0, ALU.min, ALU.mult).then_inc(nmin_done, 1)
                pool.wait_ge(nmin_done, U + 1)
                nc.gpsimd.tensor_tensor(nrm[:], nmin[:], expo[:, 1:2], ALU.pow).then_inc(nrm_done, 1)

            def low_part(U, p):
                pool.wait_ge(hi_done, U + 1)
                pool.wait_ge(dx_done, U + 1)
                nc.gpsimd.tensor_tensor(xn[p][:], xn[p][:], xhi[:].bitcast(F32), ALU.subtract).then_inc(lo_done, 1)

            def apply_gate(T, p, j, c):
                pool.wait_ge(evac_done, T + 1)
                pool.wait_ge(*read_out(f"ga1.{j}", c, back=1))
                nc.gpsimd.tensor_tensor(dx[p][:], dx[p][:], sg[p][:], ALU.mult).then_inc(yg_done, 1)

            pool.wait_ge(loaded, 16 * LOADS)
            pool.wait_ge(setup_v, SETUP_V)
            start_set(0, 0)
            pool.wait_ge(set_step, 2)
            for q in range(4):
                convolve(f"first{q}", q, 0, None)
            inverse_std(0)
            convolve("xrA.1", 0, 1, None)
            affine(0, 0)
            norm(0)
            skip_term(0, 0, 1, None)
            low_part(0, 0)
            convolve("xrB.1", 1, 1, None)
            with pool.Fori(0, SETS) as s:
                with pool.Fori(0, CPS) as k:
                    c = s * CPS + k
                    for j in range(TPC):
                        T = 2 * c + j
                        U = T + 1
                        f = c + 1 + j
                        q = 2 - 2 * j
                        apply_gate(T, 1 - j, j, c)
                        inverse_std(U)
                        if j == 1:
                            with pool.If(k == CPS - 2):
                                pool.wait_ge(conv_done, 4 * c + 8)
                                start_set(s + 1, s + 1)
                                pool.wait_ge(set_step, 2 * s + 4)
                                apart(pool)
                        affine(U, 1 - j)
                        convolve(f"xrA.{j}", q, f, c)
                        norm(U)
                        skip_term(U, 1 - j, j, c)
                        low_part(U, 1 - j)
                        convolve(f"xrB.{j}", q + 1, f, c)
            apply_gate(TILES, 1, 0, CHUNKS)

        @block.vector
        def _(dve):
            def statistics(U, p, j, c):
                dve.wait_ge(*read_out(f"tr1.{j}", c))
                nc.vector.bn_stats(bst[:, 0, :], xn[p][:, 0:HALF])
                nc.vector.bn_stats(bst[:, 1, :], xn[p][:, HALF:DI]).then_inc(stat_step, 1)
                dve.wait_ge(stat_step, 2 * U + 1)
                apart(dve)
                nc.vector.bn_aggr(mv[:], bst[:].rearrange("p a b -> p (a b)")).then_inc(stat_step, 1)
                dve.wait_ge(stat_step, 2 * U + 2)
                dve.wait_ge(rstd_done, U)
                nc.vector.tensor_scalar(ve[:], mv[:, 1:2], EPS, None, ALU.add).then_inc(ve_done, 1)

            def normalise(U, p):
                dve.wait_ge(rstd_done, U + 1)
                nc.vector.scalar_tensor_tensor(nmr[:], mv[:, 0:1], -1.0, rstd[:], ALU.mult, ALU.mult).then_inc(x3_step, 1)
                dve.wait_ge(x3_step, 5 * U + 1)
                nc.vector.tensor_scalar(xn[p][:], xn[p][:], rstd[:], nmr[:], ALU.mult, ALU.add).then_inc(xhat_done, 1)
                nc.vector.scalar_tensor_tensor(t48[:], s1[:], nmr[:], s2[:], ALU.mult, ALU.add).then_inc(x3_step, 1)

            def projections(U, j, c):
                bank, before = bank_use(f"xq.{j}", c)
                dve.wait_ge(x3_step, 5 * U + 2)
                apart(dve)
                dve.wait_ge(*filled(f"xq.{j}", c))
                nc.vector.scalar_tensor_tensor(t48[:], wb[bank][:, 0:NPROJ], rstd[:], t48[:], ALU.mult, ALU.add).then_inc(x3_step, 1)
                dve.wait_ge(x3_step, 5 * U + 3)
                nc.vector.scalar_tensor_tensor(q48[:], wb[bank][:, PROJ:PROJ + NPROJ], rstd[:], t48[:], ALU.mult, ALU.add)\
                    .then_inc(q_done, 1)
                dve.wait_ge(q_done, U + 1)
                dve.sem_inc(bank_free[bank], 1)

            def expand(U, j, c):
                dve.wait_ge(th_done, U + 1)
                dve.wait_ge(nrm_done, U + 1)
                dve.wait_ge(coef_done, U)
                nc.vector.tensor_tensor(ta[:], th[:], a2[:], ALU.mult).then_inc(x3_step, 1)
                m = msk[:].unsqueeze(2).to_broadcast([P, NB, DS])

                def wide(a):
                    return a.unsqueeze(1).to_broadcast([P, NB, DS])

                o = [x3[:, v, :].rearrange("p (b d) -> p b d", b=NB) for v in range(3)]
                nc.vector.scalar_tensor_tensor(o[0], wide(q48[:, 0:DS]), nrm[:], m, ALU.mult, ALU.mult)
                nc.vector.tensor_tensor(o[2], wide(q48[:, DS:2 * DS]), m, ALU.mult).then_inc(x3_step, 1)
                dve.wait_ge(x3_step, 5 * U + 5)
                nc.vector.scalar_tensor_tensor(o[1], wide(ta[:]), 1.0, m, ALU.add, ALU.mult).then_inc(x3_done, 1)

            def coefficients(U, p, j, c):
                bank, before = bank_use(f"sm.{j}", c)
                dve.wait_ge(bank_ready[bank], before + 1)
                dve.wait_ge(coef_done, U)
                n0 = 7 * U
                nc.vector.tensor_reduce(ba[:], wb[bank][:, 0:2 * P].rearrange("p (v n b) -> p v n b", v=2, b=NB),
                                        AX_X, ALU.add).then_inc(coef_step, 1)
                ad = ba[:, 1, :].rearrange("p (g t) -> p g t", g=NG)
                for t in range(TS):
                    dve.wait_ge(coef_step, n0 + t + 1)
                    prev = pcar[:] if t == 0 else pp[p][:, :, t - 1]
                    nc.vector.tensor_tensor(pp[p][:, :, t], prev, ad[:, :, t], ALU.mult).then_inc(coef_step, 1)
                dve.wait_ge(coef_step, n0 + 5)
                nc.vector.reciprocal(ip[:], pp[p][:].rearrange("p g t -> p (g t)")).then_inc(coef_step, 1)
                bank_c = wb[bank][:, 2 * P:3 * P].rearrange("p (g t b) -> p g t b", g=NG, t=TS)
                for t in range(TS):
                    ins = nc.vector.tensor_tensor(lhc[p][:, :, t, t * NB:(t + 1) * NB], bank_c[:, :, t, :],
                                                  pp[p][:, :, t:t + 1].to_broadcast([P, NG, NB]), ALU.mult)
                ins.then_inc(bank_free[bank], 1)
                dve.wait_ge(coef_step, n0 + 6)
                nc.vector.tensor_scalar(lim[p][:, 0, :], ip[:], CLIP, None, ALU.mult)
                nc.vector.tensor_scalar(lim[p][:, 1, :], ip[:], -CLIP, None, ALU.mult)
                nc.vector.tensor_tensor(bdp[p][:], ba[:, 0, :], ip[:], ALU.mult).then_inc(coef_step, 1)
                dve.wait_ge(coef_step, n0 + 7)
                nc.vector.tensor_copy(pcar[:], pp[p][:, :, TS - 1]).then_inc(coef_done, 1)

            def update(T, i, p):
                t, g = i // NG, i % NG
                col = g * TS + t
                dve.wait_ge(x_done, ITEMS * T + i + 1)
                if i == 0:
                    dve.wait_ge(coef_done, T + 1)
                if g == 0:
                    dve.wait_ge(y_done, TS * T + t - 1 + Y0)
                dve.wait_ge(clip_done, ITEMS * T + i + 1 + CLIP0 - 4)
                nc.vector.scalar_tensor_tensor(st[t % 2][:, g, :], px[i % 2][:], bdp[p][:, col:col + 1],
                                               st[1 - t % 2][:, g, :], ALU.mult, ALU.add).then_inc(upd_done, 1)

            def clip(T, i, p):
                t, g = i // NG, i % NG
                col = g * TS + t
                dve.wait_ge(upd_done, ITEMS * T + i + 1 + UPD0)
                nc.vector.tensor_scalar(st[t % 2][:, g, :], st[t % 2][:, g, :], lim[p][:, 0, col:col + 1],
                                        lim[p][:, 1, col:col + 1], ALU.min, ALU.max).then_inc(clip_done, 1)

            def read_y(T, p):
                dve.wait_ge(y_done, TS * T + Y0)
                dve.wait_ge(dx_done, T + 1)
                nc.vector.tensor_tensor(dx[p][:], py[:], dx[p][:], ALU.add).then_inc(evac_done, 1)

            def add_residual(T, j, c):
                bank, before = bank_use(f"ou.{j}", c)
                dve.wait_ge(bank_ready[bank], before + 1)
                dve.wait_ge(res_loaded, 16 * (T + 1))
                nc.vector.tensor_tensor(res[:], wb[bank][:], res[:], ALU.add)\
                    .then_inc(bank_free[bank], 1)

            dve.wait_ge(loaded, 16 * LOADS)
            nc.vector.memset(st[1][:, 0, 0:P], 1.0)
            nc.vector.tensor_copy(selr[:].rearrange("p a b -> p (a b)"), st[0][:, 0, :])
            nc.vector.tensor_copy(st[1][:, 1, :].rearrange("p (k x) -> p k x", k=KI), bcol[:].unsqueeze(2).to_broadcast([P, KI, P]))\
                .then_inc(setup_v, 1)
            dve.wait_ge(setup_t, 1)
            nc.vector.memset(wxg[:, :, NPROJ:PROJ], 0.0)
            nc.vector.tensor_copy(wxg[:, :, 2 * DS:3 * DS], px[0][:, 0:KI * DS].rearrange("p (k x) -> p k x", k=KI))\
                .then_inc(setup_v, 1)
            dve.wait_ge(setup_v, 2)
            raw = st[1][:, 2, 0:KI * NPROJ].rearrange("p (k x) -> p k x", k=KI)
            nc.vector.tensor_copy(raw, wxg[:, :, 0:NPROJ]).then_inc(setup_raw, 1)
            dve.wait_ge(setup_raw, 1)
            nc.vector.tensor_tensor(wxg[:, :, 0:NPROJ], raw, gcol[:].unsqueeze(2).to_broadcast([P, KI, NPROJ]), ALU.mult).then_inc(setup_v, 1)
            dve.wait_ge(setup_t, 2)
            nc.vector.tensor_copy(s1[:], px[1][:, 0:NPROJ])
            nc.vector.tensor_tensor(s2[:], px[1][:, HALF:HALF + NPROJ], s2[:], ALU.add)
            dve.wait_ge(setup_a, 1)
            nc.vector.tensor_scalar(a2[:], a2[:], -0.01, None, ALU.mult)
            nc.vector.tensor_reduce(wsum[:], wc[:], AX_X, ALU.add)
            nc.vector.tensor_scalar(wneg[:], wc[:], -1.0, None, ALU.mult)
            nc.vector.memset(expo[:, 0:1], -0.5)
            nc.vector.memset(expo[:, 1:2], 0.5)
            nc.vector.memset(dx[1][:], 0.0)
            nc.vector.memset(sg[1][:], 0.0)
            nc.vector.memset(py[:], 0.0)
            nc.vector.memset(pcar[:], 1.0)
            nc.vector.memset(lhc[0][:], 0.0)
            nc.vector.memset(lhc[1][:], 0.0).then_inc(setup_v, 1)
            nc.vector.memset(st[0][:], 0.0).then_inc(upd_done, UPD0)
            nc.vector.memset(ve[:], 0.0).then_inc(clip_done, CLIP0)
            nc.vector.memset(nmr[:], 0.0).then_inc(y_done, Y0)
            dve.wait_ge(setup_v, SETUP_V)

            statistics(0, 0, 1, None)
            normalise(0, 0)
            projections(0, 1, None)
            expand(0, 1, None)
            coefficients(0, 0, 1, None)
            with dve.Fori(0, SETS) as s:
                with dve.Fori(0, CPS) as k:
                    c = s * CPS + k
                    with dve.If(k == 0):
                        dve.wait_ge(y_done, 2 * TS * c + Y0)
                        nc.vector.memset(st[1][:], 0.0).then_inc(state_zero, 1)
                        dve.wait_ge(state_zero, s + 1)
                        apart(dve)
                    for j in range(TPC):
                        T = 2 * c + j
                        U = T + 1
                        for i in range(ITEMS):
                            if i == 2:
                                read_y(T, 1 - j)
                            if i == 4:
                                statistics(U, 1 - j, j, c)
                            if i == 6:
                                normalise(U, 1 - j)
                            if i == 8:
                                projections(U, j, c)
                            if i == 12:
                                expand(U, j, c)
                            if i == 15:
                                if j == 1:
                                    with dve.If(k == CPS - 1):
                                        dve.wait_ge(coef_done, U)
                                        nc.vector.memset(pcar[:], 1.0).then_inc(decay_reset, 1)
                                        dve.wait_ge(decay_reset, s + 1)
                                        apart(dve)
                                coefficients(U, 1 - j, j, c)
                            update(T, i, j)
                            if i >= 1:
                                clip(T, i - 1, j)
                        clip(T, ITEMS - 1, j)
                        add_residual(T, j, c)
            read_y(TILES, 1)
            add_residual(TILES, 0, CHUNKS)


SETUP_V = 4


def kernel(x, cond_2048, L0_cond_W_in, L0_cond_W_conv, L0_cond_b_conv, L0_cond_ln_g, L0_cond_ln_b, L0_cond_W_xproj,
           L0_cond_W_dt, L0_cond_b_dt, L0_cond_A_log, L0_cond_D, L0_cond_W_out):
    import numpy as np
    import concourse.bacc as bacc
    from concourse.bass_utils import run_bass_kernel_spmd

    def cols(v):
        return np.ascontiguousarray(np.asarray(v).reshape(KI, P).T)

    def rows(v, n=P):
        return np.ascontiguousarray(np.broadcast_to(np.asarray(v), (n, np.asarray(v).shape[0])))

    x = np.asarray(x)
    tiles = x.reshape(SETS, NG, NB, CPS, TPC, TS, DM).transpose(0, 3, 4, 1, 5, 2, 6).reshape(TILES, P, DM)
    xT = np.zeros((CHUNKS + 2, P, KD, CH), np.float32)
    xT[:CHUNKS] = tiles.reshape(CHUNKS, CH, KD, P).transpose(0, 3, 2, 1)
    xtok = np.zeros((TILES + 1, P, DM), np.float32)
    xtok[1:] = tiles
    temb = np.zeros((P, SETS + 1, KI, BSET), np.float32)
    temb[:, :SETS] = np.asarray(cond_2048).reshape(SETS, BSET, KI, P).transpose(3, 0, 2, 1)
    w_x = np.asarray(L0_cond_W_xproj)
    b_dt = np.zeros((P, NPROJ), np.float32)
    b_dt[:, 2 * DS:] = np.asarray(L0_cond_b_dt)
    row = np.arange(P)
    sel = np.zeros((P, 2 * TS, NB, DS), np.float32)
    sel[row, (row % 64) // NB, row % NB, :] = 1.0
    mask = np.zeros((P, NB), np.float32)
    mask[row, row % NB] = 1.0
    arrays = {
        "xT": xT, "xtok": xtok, "temb": temb,
        "w_in": np.ascontiguousarray(np.asarray(L0_cond_W_in).T.reshape(KD, P, 2 * DI).transpose(1, 0, 2)),
        "w_conv": np.ascontiguousarray(np.asarray(L0_cond_W_conv).reshape(KI, P, TAPS).transpose(1, 0, 2)),
        "b_conv": cols(L0_cond_b_conv), "ln_g": cols(L0_cond_ln_g), "ln_b": cols(L0_cond_ln_b),
        "g_rows": rows(L0_cond_ln_g), "b_rows": rows(L0_cond_ln_b), "d_rows": rows(L0_cond_D),
        "w_x": np.ascontiguousarray(w_x.T.reshape(KI, P, NPROJ).transpose(1, 0, 2)),
        "w_x3": np.ascontiguousarray(w_x[2 * DS:]),
        "w_dt": np.ascontiguousarray(np.asarray(L0_cond_W_dt).T),
        "b_dt": b_dt, "a_log": rows(L0_cond_A_log),
        "w_out": np.ascontiguousarray(np.asarray(L0_cond_W_out).T.reshape(KI, P, DM).transpose(1, 0, 2)),
        "ident": np.eye(P, dtype=np.float32), "sel": sel.reshape(P, 2 * TS, P), "mask": mask,
    }
    nc = bacc.Bacc("TRN2", target_bir_lowering=False, num_devices=1, dynamic_dma_scratch_size=1024)
    aps = [nc.dram_tensor(f"in_{n}", a.shape, mybir.dt.from_np(a.dtype), kind="ExternalInput").ap() for n, a in arrays.items()]
    order = dict(zip(arrays, aps))
    result = nc.dram_tensor("out", (TILES + 1, P, DM), F32, kind="ExternalOutput").ap()
    build(nc, out=result, **order)
    r = run_bass_kernel_spmd(nc, [{f"in_{n}": a for n, a in arrays.items()}], core_ids=[0])
    got = r.results[0]["out"]
    return np.ascontiguousarray(
        got[1:].reshape(SETS, CPS, TPC, NG, TS, NB, DM).transpose(0, 3, 5, 1, 2, 4, 6).reshape(BATCH, SEQ, DM))
```

```python
from contextlib import ExitStack

import concourse.bass as bass
from concourse import mybir

F32 = mybir.dt.float32
F32R = mybir.dt.float32r
BF16 = mybir.dt.bfloat16
ALU = mybir.AluOpType
ACT = mybir.ActivationFunctionType
AX_X = mybir.AxisListType.X

P = 128
BATCH, SEQ, DM, DI, DS = 128, 128, 512, 1024, 16
NB, TS, NG = 8, 4, 4
BSET = NG * NB
SETS = BATCH // BSET
TPC = 2
CH = TPC * P
CPS = SEQ // (TS * TPC)
CHUNKS = SETS * CPS
TILES = CHUNKS * TPC
KD = DM // P
KI = DI // P
HALF = 512
ITEMS = TS * NG
TAPS = 4
CLIP = 10.0
EPS = 1e-5
NPROJ = 3 * DS
PROJ = 64

HALVES = {
    0: ["tr0", "tr1", "xp", "ot0", "ot1", "xq", "ou"],
    1: ["ga0", "xrA", "xrB", "sm", "ga1"],
}
BODY = {b: [f"{u}.{j}" for j in range(TPC) for u in HALVES[b]] for b in HALVES}
BEFORE = {b: [f"first{b}", f"first{b + 2}"] + [f"{u}.1" for u in HALVES[b] if u not in ("ot0", "ot1", "ou")]
          for b in HALVES}
AFTER = {0: ["ot0.0", "ot1.0", "ou.0"], 1: []}


def bank_use(name, c):
    last = isinstance(c, int) and c == CHUNKS
    for bank in (0, 1):
        order = BEFORE[bank] if c is None else AFTER[bank] if last else BODY[bank]
        if name in order:
            if c is None:
                return bank, order.index(name)
            return bank, c * len(BODY[bank]) + (len(BEFORE[bank]) + order.index(name))
    raise KeyError(name)


def build(nc, xT, xtok, temb, w_in, w_conv, b_conv, ln_g, ln_b, g_rows, b_rows, d_rows, w_x, w_x3,
          w_dt, b_dt, a_log, w_out, ident, sel, mask, out):
    with ExitStack() as ctx:
        def sb(name, shape, dt=F32):
            return ctx.enter_context(nc.sbuf_tensor(name, shape, dt))

        def psum(name, shape):
            return ctx.enter_context(nc.psum_tensor(name, shape, F32))

        def sem(name):
            return ctx.enter_context(nc.semaphore(name))

        win = sb("win", [P, KD, 2 * DI])
        wo_hi = sb("wo_hi", [P, KI, DM], F32R)
        wo_lo = sb("wo_lo", [P, KI, DM], F32R)
        wxg = sb("wxg", [P, KI, PROJ])
        wc = sb("wc", [P, KI, TAPS])
        wsum = sb("wsum", [P, KI])
        bc = sb("bc", [P, KI])
        gcol = sb("gcol", [P, KI])
        bcol = sb("bcol", [P, KI])
        grow = sb("grow", [P, DI])
        brow = sb("brow", [P, DI])
        drow = sb("drow", [P, DI])
        te = sb("te", [P, KI, BSET])
        idn = sb("idn", [P, P])
        selr = sb("selr", [P, 8, P], F32R)
        msk = sb("msk", [P, NB])
        s1 = sb("s1", [P, NPROJ])
        s2 = sb("s2", [P, NPROJ])
        a2 = sb("a2", [P, DS])
        expo = sb("expo", [P, 3])
        wdt = sb("wdt", [DS, DS])
        xt = sb("xt", [P, KD, CH])
        xg = sb("xg", [P, KD, CH])
        tap0 = sb("tap0", [P, KI, NG, NB * TS * TPC])
        later = [[sb(f"later{b}_{s}", [P, 2, NG, NB * (s + TS * TPC)]) for s in range(1, TAPS)] for b in range(2)]
        cterm = sb("cterm", [P, KI, BSET])
        last = sb("last", [P, KI, NG, NB * (TAPS - 1)])
        xct = [sb(f"xct{p}", [P, KI, P]) for p in range(2)]
        xn = [sb(f"xn{p}", [P, DI]) for p in range(2)]
        xhi = sb("xhi", [P, DI], F32R)
        stack = [sb(f"stack{p}", [P, 2, DI], F32R) for p in range(2)]
        dx = [sb(f"dx{p}", [P, DI]) for p in range(2)]
        sg = [sb(f"sg{p}", [P, DI]) for p in range(2)]
        sums = sb("sums", [P, 2])
        nmean = sb("nmean", [P, 1])
        ssq = sb("ssq", [P, 1])
        ve = sb("ve", [P, 1])
        rstd = sb("rstd", [P, 1])
        nmr = sb("nmr", [P, 1])
        t48 = sb("t48", [P, NPROJ])
        q48 = sb("q48", [P, NPROJ])
        pq = sb("pq", [P, P])
        th = sb("th", [P, DS])
        ta = sb("ta", [P, DS])
        nsq = sb("nsq", [P, 1])
        nmin = sb("nmin", [P, 1])
        nrm = sb("nrm", [P, 1])
        x3 = sb("x3", [P, 3, P])
        ba = sb("ba", [P, 2, ITEMS])
        pcar = sb("pcar", [P, NG])
        pp = [sb(f"pp{p}", [P, NG, TS]) for p in range(2)]
        ip = sb("ip", [P, ITEMS])
        lim = [sb(f"lim{p}", [P, 2, ITEMS]) for p in range(2)]
        bdp = [sb(f"bdp{p}", [P, ITEMS]) for p in range(2)]
        lhc = [sb(f"lhc{p}", [P, NG, TS, BSET]) for p in range(2)]
        st = [sb(f"st{p}", [P, NG, DI]) for p in range(2)]
        wx3 = st[1][0:DS, 3, :]
        yt_hi = sb("yt_hi", [P, KI, P], F32R)
        yt_lo = sb("yt_lo", [P, KI, P], F32R)
        res = sb("res", [P, DM])

        px = [psum(f"px{p}", [P, DI]) for p in range(2)]
        py = psum("py", [P, DI])
        wb = [psum(f"wb{p}", [P, HALF]) for p in range(2)]

        loaded = sem("loaded")
        win_loaded = sem("win_loaded")
        late_loaded = sem("late_loaded")
        setup_v = sem("setup_v")
        setup_t = sem("setup_t")
        setup_a = sem("setup_a")
        setup_raw = sem("setup_raw")
        te_loaded = sem("te_loaded")
        xt_loaded = sem("xt_loaded")
        xg_loaded = [sem(f"xg_loaded{t}") for t in range(TPC)]
        bank_ready = [sem(f"bank_ready{p}") for p in range(2)]
        bank_free = [sem(f"bank_free{p}") for p in range(2)]
        conv_step = sem("conv_step")
        conv_done = sem("conv_done")
        last_kept = sem("last_kept")
        last_scaled = sem("last_scaled")
        last_set = sem("last_set")
        yt_split = sem("yt_split")
        wo_rounded = sem("wo_rounded")
        set_step = sem("set_step")
        silu_done = sem("silu_done")
        stat_step = sem("stat_step")
        mean_done = sem("mean_done")
        ssq_done = sem("ssq_done")
        rstd_done = sem("rstd_done")
        xhat_done = sem("xhat_done")
        q_done = sem("q_done")
        aff_step = sem("aff_step")
        xn_done = sem("xn_done")
        th_done = sem("th_done")
        nsq_done = sem("nsq_done")
        nmin_done = sem("nmin_done")
        nrm_done = sem("nrm_done")
        hi_done = sem("hi_done")
        dx_done = sem("dx_done")
        lo_done = sem("lo_done")
        stacked = sem("stacked")
        x3_step = sem("x3_step")
        x3_done = sem("x3_done")
        coef_step = sem("coef_step")
        coef_done = sem("coef_done")
        x_done = sem("x_done")
        upd_done = sem("upd_done")
        shared_scaled = sem("shared_scaled")
        shared_done = sem("shared_done")
        clip_done = sem("clip_done")
        y_done = sem("y_done")
        state_zero = sem("state_zero")
        decay_reset = sem("decay_reset")
        evac_done = sem("evac_done")
        yg_done = sem("yg_done")
        res_loaded = sem("res_loaded")
        stored = sem("stored")

        OWN = TPC * ITEMS - 1
        UPD0 = 1
        SCALED0 = 1
        CLIP0 = 4
        Y0 = 2
        STORED0 = 16

        def apart(eng):
            eng.nop(nofuse=True)

        def vacant(name, c):
            bank, before = bank_use(name, c)
            return bank_free[bank], before

        def filled(name, c):
            bank, before = bank_use(name, c)
            return bank_ready[bank], before + 1

        def read_out(name, c):
            bank, before = bank_use(name, c)
            return bank_free[bank], before + 1

        LOADS = 13
        LATE_LOADS = 4

        block = ctx.enter_context(nc.Block())

        @block.sync
        def _(sp):
            for dst, src in ((idn, ident), (wx3, w_x3), (wdt, w_dt), (wc, w_conv), (bc, b_conv), (gcol, ln_g),
                             (bcol, ln_b), (wxg[:, :, 0:NPROJ], w_x), (s2, b_dt), (a2, a_log), (msk, mask), (te, temb[0]),
                             (sg[0][:].rearrange("p (a b) -> p a b", a=8), sel)):
                sp.dma_start(dst[:], src).then_inc(loaded, 16)
            sp.dma_start(win[:], w_in).then_inc(win_loaded, 16)

            def load_chunk(f, c):
                if c is not None:
                    sp.wait_ge(*read_out("xrB.0", c))
                for t in range(TPC):
                    sp.wait_ge(xg_loaded[t], 16 * f)
                sp.dma_start(xt[:], xT[f]).then_inc(xt_loaded, 16)

            def keep_for_gates(t, f, c):
                sp.wait_ge(xt_loaded, 16 * f + 16)
                if c is not None:
                    sp.wait_ge(*read_out(f"ga1.{1 - t}", c - 1 if t == 0 else c))
                cols = slice(t * P, (t + 1) * P)
                sp.dma_start(xg[:, :, cols], xt[:, :, cols]).then_inc(xg_loaded[t], 16)

            def stack_parts(U, p, c):
                sp.wait_ge(hi_done, U + 1)
                apart(sp)
                if p == 1 or c is not None:
                    sp.wait_ge(x_done, ITEMS * (U - 1) + 1)
                st32 = stack[p][:].bitcast(F32)
                for part, src, rows in ((0, xhi[:].bitcast(F32), slice(0, 64)), (1, xn[p], slice(64, 128))):
                    if part == 1:
                        sp.wait_ge(lo_done, U + 1)
                        apart(sp)
                    for pair in range(2):
                        sp.dma_start(st32[rows, pair, :], src[64 * pair:64 * pair + 64, :]).then_inc(stacked, 16)

            def load_temb(s):
                sp.wait_ge(last_set, 4 * s)
                apart(sp)
                sp.wait_ge(set_step, 2 * s)
                apart(sp)
                sp.dma_start(te[:], temb[s]).then_inc(te_loaded, 16)

            def load_residual(T):
                sp.wait_ge(stored, 16 * T + STORED0)
                sp.dma_start(res[:], xtok[T]).then_inc(res_loaded, 16)

            def store(T, j, c):
                sp.wait_ge(*read_out(f"ou.{j}", c))
                sp.dma_start(out[T], res[:]).then_inc(stored, 16)

            sp.sem_inc(stored, STORED0)
            load_chunk(0, None)
            keep_for_gates(0, 0, None)
            keep_for_gates(1, 0, None)
            for dst, src in ((st[0][:].rearrange("p a b -> p (a b)").rearrange("p (k x) -> p k x", k=KI), w_out),
                             (grow, g_rows), (brow, b_rows), (drow, d_rows)):
                sp.dma_start(dst[:], src).then_inc(late_loaded, 16)
            sp.wait_ge(*read_out("first3", None))
            load_chunk(1, None)
            load_temb(1)
            stack_parts(0, 0, None)
            with sp.Fori(0, SETS) as s:
                with sp.Fori(0, CPS) as k:
                    c = s * CPS + k
                    load_residual(2 * c)
                    keep_for_gates(0, c + 1, c)
                    stack_parts(2 * c + 1, 1, c)
                    store(2 * c, 0, c)
                    load_residual(2 * c + 1)
                    keep_for_gates(1, c + 1, c)
                    load_chunk(c + 2, c)
                    stack_parts(2 * c + 2, 0, c)
                    store(2 * c + 1, 1, c)
                load_temb(s + 2)
            load_residual(TILES)
            store(TILES, 0, CHUNKS)
            sp.wait_ge(stored, 16 * (TILES + 1) + STORED0)
            sp.wait_ge(te_loaded, 16 * (SETS + 1))

        @block.tensor
        def _(pe):
            def input_blocks(name, q, part, f, c):
                bank, _ = bank_use(name, c)
                if part == 0:
                    pe.wait_ge(*vacant(name, c))
                    if q in (0, 2):
                        pe.wait_ge(xt_loaded, 16 * f + 16)
                blk = 2 * q + part
                for kd in range(KD):
                    mm = nc.tensor.matmul(wb[bank][:, part * CH:(part + 1) * CH], win[:, kd, blk * P:(blk + 1) * P],
                                          xt[:, kd, :], start=(kd == 0), stop=(kd == KD - 1))
                if part == 1:
                    mm.then_inc(bank_ready[bank], 1)

            def turn_xc(h, U, p, j, c):
                bank, _ = bank_use(f"tr{h}.{j}", c)
                ps = wb[bank]
                pe.wait_ge(*vacant(f"tr{h}.{j}", c))
                pe.wait_ge(silu_done, U + 1)
                for b in range(4):
                    mm = nc.tensor.transpose(ps[:, b * P:(b + 1) * P], xct[p][:, 4 * h + b, :], idn[:])
                mm.then_inc(bank_ready[bank], 1)

            def project_bcd(U, p, j, c):
                bank, _ = bank_use(f"xp.{j}", c)
                pe.wait_ge(*vacant(f"xp.{j}", c))
                for b in range(4):
                    for h in range(2):
                        mm = nc.tensor.matmul(wb[bank][PROJ * h:PROJ * (h + 1), 0:P], wxg[:, 4 * h + b, :],
                                              xct[p][:, 4 * h + b, :], start=(b == 0), stop=(b == 3),
                                              tile_position=(0, PROJ * h))
                mm.then_inc(bank_ready[bank], 1)

            def turn_bcd(U, j, c):
                bank, _ = bank_use(f"xq.{j}", c)
                pe.wait_ge(*vacant(f"xq.{j}", c))
                pe.wait_ge(*read_out(f"xp.{j}", c))
                nc.tensor.transpose(wb[bank][:, 0:P], pq[:], idn[:]).then_inc(bank_ready[bank], 1)

            def gate(h, part, U, p, j, c):
                if part == 0:
                    pe.wait_ge(*vacant(f"ga{h}.{j}", c))
                    pe.wait_ge(xg_loaded[1 - j], 16 * (c + 1 + j) if c is not None else 16)
                bank, _ = bank_use(f"ga{h}.{j}", c)
                src = xg[:, :, (1 - j) * P:(2 - j) * P]
                for kd in (2 * part, 2 * part + 1):
                    mm = nc.tensor.matmul(wb[bank][:], src[:, kd, :],
                                          win[:, kd, DI + h * HALF:DI + (h + 1) * HALF], start=(kd == 0), stop=(kd == KD - 1))
                if part == 1:
                    mm.then_inc(bank_ready[bank], 1)

            def turn_coefs(U, j, c):
                bank, _ = bank_use(f"sm.{j}", c)
                ps = wb[bank]
                pe.wait_ge(*vacant(f"sm.{j}", c))
                pe.wait_ge(x3_done, U + 1)
                for v in range(3):
                    mm = nc.tensor.transpose(ps[:, v * P:(v + 1) * P], x3[:, v, :], idn[:])
                mm.then_inc(bank_ready[bank], 1)

            def spread(T, i, p, c):
                if i == 0:
                    pe.wait_ge(stacked, 64 * (T + 1))
                t, g = i // NG, i % NG
                if p == 0 and i == 1:
                    pe.wait_ge(shared_scaled, c + SCALED0)
                elif p == 0:
                    pe.wait_ge(upd_done, OWN * c + max(i - 1, 0) + UPD0)
                else:
                    pe.wait_ge(upd_done, OWN * c + ITEMS + i - 1 + UPD0)
                for h in range(2):
                    mm = nc.tensor.matmul(px[i % 2][:, h * HALF:(h + 1) * HALF], selr[:, (g % 2) * TS + t, :],
                                          stack[p][:, g // 2, h * HALF:(h + 1) * HALF], start=True, stop=True)
                mm.then_inc(x_done, 1)

            def contract(T, t, p):
                if t == 0:
                    pe.wait_ge(coef_done, T + 1)
                    pe.wait_ge(evac_done, T + 1)
                pe.wait_ge(clip_done, ITEMS * T + NG * t + NG + CLIP0)
                for h in range(2):
                    for g in range(NG):
                        mm = nc.tensor.matmul(py[g * BSET:(g + 1) * BSET, h * HALF:(h + 1) * HALF], lhc[p][:, g, t, :],
                                              st[t % 2][:, g, h * HALF:(h + 1) * HALF],
                                              start=(t == 0), stop=(t == TS - 1), tile_position=(0, g * BSET))
                mm.then_inc(y_done, 1)

            def turn_yg(h, T, j, c):
                bank, _ = bank_use(f"ot{h}.{j}", c)
                ps = wb[bank]
                pe.wait_ge(*vacant(f"ot{h}.{j}", c))
                pe.wait_ge(yg_done, T + 1)
                for b in range(4):
                    mm = nc.tensor.transpose(ps[:, b * P:(b + 1) * P], dx[1 - j][:, (4 * h + b) * P:(4 * h + b + 1) * P], idn[:])
                mm.then_inc(bank_ready[bank], 1)

            def project_out(part, T, j, c):
                if part == 0:
                    pe.wait_ge(*vacant(f"ou.{j}", c))
                    pe.wait_ge(yt_split, T + 1)
                bank, _ = bank_use(f"ou.{j}", c)
                for blk in (2 * part, 2 * part + 1):
                    for a, b in ((yt_hi, wo_hi), (yt_hi, wo_lo), (yt_lo, wo_hi)):
                        mm = nc.tensor.matmul(wb[bank][:], a[:, blk, :], b[:, blk, :], start=(blk == 0 and b is wo_hi and a is yt_hi),
                                              stop=(blk == KI - 1 and a is yt_lo))
                if part == 3:
                    mm.then_inc(bank_ready[bank], 1)

            pe.wait_ge(loaded, 16 * LOADS)
            for blk in range(KI):
                mm = nc.tensor.matmul(px[0][:, blk * DS:(blk + 1) * DS], wx3[:, blk * P:(blk + 1) * P], wdt[:],
                                      start=True, stop=True)
            mm.then_inc(setup_t, 1)
            pe.wait_ge(setup_v, 3)
            for blk in range(KI):
                nc.tensor.matmul(px[1][:, 0:NPROJ], st[1][:, 0, 0:P], wxg[:, blk, 0:NPROJ], start=(blk == 0), stop=(blk == KI - 1))
            for blk in range(KI):
                mm = nc.tensor.matmul(px[1][:, HALF:HALF + NPROJ], st[1][:, 1, blk * P:(blk + 1) * P],
                                      st[1][:, 2, blk * NPROJ:(blk + 1) * NPROJ], start=(blk == 0), stop=(blk == KI - 1))
            mm.then_inc(setup_t, 1)

            def front(n, U, p, j, c):
                if n in (1, 2):
                    turn_xc(n - 1, U, p, j, c)
                if n == 3:
                    project_bcd(U, p, j, c)
                if n in GATE0_AT:
                    gate(0, GATE0_AT.index(n), U, p, j, c)
                if n == 7:
                    turn_bcd(U, j, c)
                if n == 13:
                    turn_coefs(U, j, c)
                if n == 15:
                    gate(1, 0, U, p, j, c)

            def convs(n, f, j, c):
                if n in XRA_AT:
                    input_blocks(f"xrA.{j}", 2 - 2 * j, XRA_AT.index(n), f, c)
                if n in XRB_AT:
                    input_blocks(f"xrB.{j}", 3 - 2 * j, XRB_AT.index(n), f, c)

            GATE0_AT = (2, 3)
            XRA_AT = (5, 6)
            XRB_AT = (9, 10)
            OUT_AT = (11, 12, 13, 14)
            pe.wait_ge(win_loaded, 16)
            for q in range(4):
                for part in range(2):
                    input_blocks(f"first{q}", q, part, 0, None)
            pe.wait_ge(setup_v, SETUP_V)
            for n in range(ITEMS):
                front(n, 0, 0, 1, None)
                convs(n, 1, 1, None)
            pe.wait_ge(clip_done, CLIP0)
            for h in range(2):
                for g in range(NG):
                    nc.tensor.matmul(py[g * BSET:(g + 1) * BSET, h * HALF:(h + 1) * HALF], lhc[1][:, g, 0, :],
                                     st[1][:, g, h * HALF:(h + 1) * HALF], start=True, stop=False,
                                     tile_position=(0, g * BSET))
            spread(0, 0, 0, 0)
            spread(0, 1, 0, 0)
            with pe.Fori(0, SETS) as s:
                with pe.Fori(0, CPS) as k:
                    c = s * CPS + k
                    for j in range(TPC):
                        T = 2 * c + j
                        for n in range(ITEMS):
                            if n == 0:
                                contract(T - 1, TS - 1, 1 - j)
                            if n + 2 < ITEMS:
                                spread(T, n + 2, j, c)
                            else:
                                spread(T + 1, n + 2 - ITEMS, 1 - j, c + j)
                            if n in (4, 6):
                                turn_yg((n - 4) // 2, T, j, c)
                            front(n, T + 1, 1 - j, j, c)
                            if n == 1:
                                gate(1, 1, T, j, 1 - j, c - 1 if j == 0 else c)
                            convs(n, c + 1 + j, j, c)
                            if n in OUT_AT:
                                project_out(OUT_AT.index(n), T, j, c)
                            if n % NG == 0 and n > 0:
                                contract(T, n // NG - 1, j)
            contract(TILES - 1, TS - 1, 1)
            gate(1, 1, TILES, 0, 1, CHUNKS - 1)
            for h in range(2):
                turn_yg(h, TILES, 0, CHUNKS)
            for part in range(4):
                project_out(part, TILES, 0, CHUNKS)

        @block.scalar
        def _(act):
            def start_last(q, s):
                n = 4 * s + q
                if not isinstance(s, int):
                    act.wait_ge(last_kept, 4 * CPS * s + q + 1 - 4)
                for t in range(TAPS - 1):
                    ins = nc.scalar.activation(last[:, 2 * q:2 * q + 2, :, NB * t:NB * (t + 1)].rearrange("p k g b -> p (k g) b"),
                                               te[:, 2 * q:2 * q + 2, :].rearrange("p k (g b) -> p (k g) b", g=NG),
                                               ACT.Copy, scale=-1.0)
                ins.then_inc(last_set, 1)
                act.wait_ge(last_set, n + 1)
                apart(act)

            def scale_last(q, f):
                if not isinstance(f, int) or 4 * f + q >= 2:
                    act.wait_ge(conv_done, 4 * f + q - 1)
                if not isinstance(f, int) or f > 0:
                    act.wait_ge(last_kept, 4 * f + q - 3)
                for part in range(2):
                    blk = 2 * q + part
                    for tap in range(1, TAPS):
                        ins = nc.scalar.activation(later[q % 2][tap - 1][:, part, :, 0:NB * tap],
                                                   last[:, blk, :, NB * (TAPS - 1 - tap):],
                                                   ACT.Copy, scale=wc[:, blk, TAPS - 1 - tap:TAPS - tap])
                ins.then_inc(last_scaled, 1)

            def scale_taps(name, q, f, c):
                bank, _ = bank_use(name, c)
                act.wait_ge(*filled(name, c))
                act.wait_ge(last_scaled, 4 * f + q + 1)
                src = wb[bank][:].rearrange("p (i j g x) -> p i g j x", i=2, j=TPC, g=NG)
                nc.scalar.activation(last[:, 2 * q:2 * q + 2, :, :], src[:, :, :, TPC - 1, NB * (TS - TAPS + 1):], ACT.Copy)\
                    .then_inc(last_kept, 1)
                for part in range(2):
                    blk = 2 * q + part
                    for tap in range(TAPS):
                        dst = tap0[:, blk, :, :] if tap == 0 else later[q % 2][tap - 1][:, part, :, NB * tap:]
                        ins = nc.scalar.activation(dst.rearrange("p g (j x) -> p g j x", j=TPC), src[:, part, :, :, :], ACT.Copy,
                                                   scale=wc[:, blk, TAPS - 1 - tap:TAPS - tap])
                ins.then_inc(bank_free[bank], 1)

            def silu_tile(p, f, c):
                act.wait_ge(conv_done, 4 * f + 4)
                if c is not None:
                    act.wait_ge(yt_split, 2 * f - 1)
                src = tap0[:, :, :, p * TS * NB:(p + 1) * TS * NB].rearrange("p k g x -> p (k g) x")
                nc.scalar.activation(xct[p][:].rearrange("p k (g x) -> p (k g) x", g=NG), src, ACT.Silu).then_inc(silu_done, 1)

            def copy_xc(h, U, p, j, c):
                bank, before = bank_use(f"tr{h}.{j}", c)
                act.wait_ge(bank_ready[bank], before + 1)
                act.wait_ge(stacked, 64 * U)
                nc.scalar.activation(xn[p][:, h * HALF:(h + 1) * HALF], wb[bank][:], ACT.Copy, accum_out=sums[:, h:h + 1])\
                    .then_inc(bank_free[bank], 1)

            def square_deviations(U, p):
                act.wait_ge(mean_done, U + 1)
                act.wait_ge(stacked, 64 * U)
                nc.scalar.activation(xhi[:].bitcast(F32), xn[p][:], ACT.Square, bias=nmean[:], accum_out=ssq[:]).then_inc(ssq_done, 1)

            def normalise(U, p):
                act.wait_ge(rstd_done, U + 1)
                nc.scalar.activation(xn[p][:], xn[p][:], ACT.Identity, bias=nmr[:], scale=rstd[:]).then_inc(xhat_done, 1)

            def copy_bcd(U, j, c):
                bank, before = bank_use(f"xp.{j}", c)
                act.wait_ge(*filled(f"xp.{j}", c))
                act.wait_ge(x3_done, U)
                nc.scalar.activation(pq[:], wb[bank][:, 0:P], ACT.Copy).then_inc(bank_free[bank], 1)

            def tanh_dt(U, j, c):
                act.wait_ge(q_done, U + 1)
                act.wait_ge(x3_done, U)
                nc.scalar.activation(th[:], q48[:, 2 * DS:3 * DS], ACT.Tanh).then_inc(th_done, 1)

            def silu_gate(h, U, p, j, c):
                bank, before = bank_use(f"ga{h}.{j}", c)
                act.wait_ge(bank_ready[bank], before + 1)
                act.wait_ge(yg_done, U)
                nc.scalar.activation(sg[p][:, h * HALF:(h + 1) * HALF], wb[bank][:], ACT.Silu)\
                    .then_inc(bank_free[bank], 1)

            def square_and_high(U, p):
                act.wait_ge(xn_done, U + 1)
                act.wait_ge(nmin_done, U)
                act.wait_ge(ssq_done, U + 1)
                nc.scalar.activation(xhi[:].bitcast(F32), xn[p][:], ACT.Square, accum_out=nsq[:]).then_inc(nsq_done, 1)
                act.wait_ge(nsq_done, U + 1)
                nc.scalar.activation(xhi[:], xn[p][:], ACT.Copy).then_inc(hi_done, 1)

            def copy_yg(h, T, j, c):
                bank, before = bank_use(f"ot{h}.{j}", c)
                act.wait_ge(bank_ready[bank], before + 1)
                act.wait_ge(stored, 16 * T + STORED0)
                src = wb[bank][:].rearrange("p (k x) -> p k x", k=4)
                nc.scalar.activation(xct[1 - j][:, 4 * h:4 * h + 4, :], src, ACT.Copy)
                nc.scalar.activation(yt_hi[:, 4 * h:4 * h + 4, :], src, ACT.Copy)\
                    .then_inc(bank_free[bank], 1)

            def scale_x(T, p):
                col = NG * TS - 1
                act.wait_ge(x_done, ITEMS * (T + 1))
                act.wait_ge(coef_done, T + 1)
                act.wait_ge(y_done, TS * T + TS - 2 + Y0)
                act.wait_ge(clip_done, ITEMS * T + ITEMS - 4 + CLIP0)
                nc.scalar.activation(st[1][:, NG - 1, :], px[1][:], ACT.Copy, scale=bdp[p][:, col:col + 1]).then_inc(shared_scaled, 1)

            act.sem_inc(shared_scaled, SCALED0)
            act.wait_ge(loaded, 16 * LOADS)
            nc.scalar.activation(a2[:], a2[:], ACT.Tanh).then_inc(setup_a, 1)
            for q in range(4):
                start_last(q, 0)
                scale_last(q, 0)
                scale_taps(f"first{q}", q, 0, None)
            act.wait_ge(late_loaded, 16 * LATE_LOADS)
            nc.scalar.activation(wo_hi[:].rearrange("p k x -> p (k x)"), st[0][:].rearrange("p a b -> p (a b)"), ACT.Copy).then_inc(wo_rounded, 1)
            silu_tile(0, 0, None)
            silu_tile(1, 0, None)
            act.wait_ge(setup_v, SETUP_V)
            copy_xc(0, 0, 0, 1, None)
            copy_xc(1, 0, 0, 1, None)
            copy_bcd(0, 1, None)
            square_deviations(0, 0)
            silu_gate(0, 0, 0, 1, None)
            normalise(0, 0)
            scale_last(0, 1)
            square_and_high(0, 0)
            scale_taps("xrA.1", 0, 1, None)
            tanh_dt(0, 1, None)
            scale_last(1, 1)
            scale_taps("xrB.1", 1, 1, None)
            with act.Fori(0, SETS) as s:
                with act.Fori(0, CPS) as k:
                    c = s * CPS + k
                    for j in range(TPC):
                        T = 2 * c + j
                        U = T + 1
                        f = c + 1 + j
                        q = 2 - 2 * j
                        copy_xc(0, U, 1 - j, j, c)
                        silu_gate(1, T, j, 1 - j, c - 1 if j == 0 else c)
                        copy_xc(1, U, 1 - j, j, c)
                        copy_bcd(U, j, c)
                        square_deviations(U, 1 - j)
                        silu_gate(0, U, 1 - j, j, c)
                        normalise(U, 1 - j)
                        copy_yg(0, T, j, c)
                        with act.If(k == CPS - 1 - j):
                            act.wait_ge(te_loaded, 16 * (s + 1))
                            start_last(q, s + 1)
                            start_last(q + 1, s + 1)
                        scale_last(q, f)
                        copy_yg(1, T, j, c)
                        scale_taps(f"xrA.{j}", q, f, c)
                        square_and_high(U, 1 - j)
                        tanh_dt(U, j, c)
                        scale_last(q + 1, f)
                        scale_taps(f"xrB.{j}", q + 1, f, c)
                        if j == 1:
                            scale_x(T, j)
                        if j == 0:
                            silu_tile(0, f, c)
                            silu_tile(1, f, c)
            copy_yg(0, TILES, 0, CHUNKS)
            copy_yg(1, TILES, 0, CHUNKS)

        @block.gpsimd
        def _(pool):
            def start_set(n):
                nc.gpsimd.tensor_tensor(cterm[:], te[:], wsum[:].unsqueeze(2).to_broadcast([P, KI, BSET]), ALU.mult)\
                    .then_inc(set_step, 1)
                pool.wait_ge(set_step, 2 * n + 1)
                nc.gpsimd.tensor_tensor(cterm[:], cterm[:], bc[:].unsqueeze(2).to_broadcast([P, KI, BSET]), ALU.add)\
                    .then_inc(set_step, 1)

            def convolve(name, q, f, c):
                pool.wait_ge(*read_out(name, c))
                ks = slice(2 * q, 2 * q + 2)
                n = TPC * TS * NB
                acc = tap0[:, ks, :, :].rearrange("p k g x -> p (k g) x")
                for tap in range(1, TAPS):
                    nc.gpsimd.tensor_tensor(acc, acc, later[q % 2][tap - 1][:, :, :, 0:n].rearrange("p k g x -> p (k g) x"), ALU.add)\
                        .then_inc(conv_step, 1)
                    pool.wait_ge(conv_step, (4 * f + q) * 3 + tap)
                acc4 = tap0[:, ks, :, :].rearrange("p k g (t b) -> p (k g) t b", b=NB)
                ct = cterm[:, ks, :].rearrange("p k (g b) -> p (k g) b", g=NG).unsqueeze(2)\
                    .to_broadcast([P, 2 * NG, TPC * TS, NB])
                nc.gpsimd.tensor_tensor(acc4, acc4, ct, ALU.add).then_inc(conv_done, 1)

            def mean(U, j, c):
                pool.wait_ge(*read_out(f"tr1.{j}", c))
                nc.gpsimd.tensor_tensor(nmean[:], sums[:, 0:1], sums[:, 1:2], ALU.add).then_inc(stat_step, 1)
                pool.wait_ge(stat_step, 3 * U + 1)
                nc.gpsimd.tensor_tensor(nmean[:], nmean[:], expo[:, 2:3], ALU.mult).then_inc(mean_done, 1)

            def inverse_std(U):
                pool.wait_ge(ssq_done, U + 1)
                apart(pool)
                nc.gpsimd.tensor_scalar(ve[:], ssq[:], 1.0 / DI, EPS, ALU.mult, ALU.add).then_inc(stat_step, 1)
                pool.wait_ge(stat_step, 3 * U + 2)
                pool.wait_ge(x3_done, U)
                nc.gpsimd.tensor_tensor(rstd[:], ve[:], expo[:, 0:1], ALU.pow).then_inc(stat_step, 1)
                pool.wait_ge(stat_step, 3 * U + 3)
                nc.gpsimd.tensor_tensor(nmr[:], nmean[:], rstd[:], ALU.mult).then_inc(rstd_done, 1)

            def affine(U, p):
                pool.wait_ge(xhat_done, U + 1)
                nc.gpsimd.tensor_tensor(xn[p][:], xn[p][:], grow[:], ALU.mult).then_inc(aff_step, 1)
                pool.wait_ge(aff_step, U + 1)
                nc.gpsimd.tensor_tensor(xn[p][:], xn[p][:], brow[:], ALU.add).then_inc(xn_done, 1)

            def skip_term(U, p, j, c):
                pool.wait_ge(xn_done, U + 1)
                if c is not None:
                    pool.wait_ge(*read_out(f"ot1.{j}", c))
                nc.gpsimd.tensor_tensor(dx[p][:], xn[p][:], drow[:], ALU.mult).then_inc(dx_done, 1)

            def norm(U):
                pool.wait_ge(nsq_done, U + 1)
                pool.wait_ge(x3_done, U)
                apart(pool)
                nc.gpsimd.tensor_scalar(nmin[:], nsq[:], 1.0, 1.0, ALU.min, ALU.mult).then_inc(nmin_done, 1)
                pool.wait_ge(nmin_done, U + 1)
                nc.gpsimd.tensor_tensor(nrm[:], nmin[:], expo[:, 1:2], ALU.pow).then_inc(nrm_done, 1)

            def low_part(U, p):
                pool.wait_ge(hi_done, U + 1)
                pool.wait_ge(dx_done, U + 1)
                nc.gpsimd.tensor_tensor(xn[p][:], xn[p][:], xhi[:].bitcast(F32), ALU.subtract).then_inc(lo_done, 1)

            def split_yt(T, j, c):
                pool.wait_ge(*read_out(f"ot1.{j}", c))
                if not isinstance(T, int):
                    pool.wait_ge(stored, 16 * T + STORED0)
                nc.gpsimd.tensor_tensor(yt_lo[:], xct[1 - j][:], yt_hi[:].bitcast(F32), ALU.subtract).then_inc(yt_split, 1)

            def add_state(c):
                pool.wait_ge(shared_scaled, c + 1 + SCALED0)
                nc.gpsimd.tensor_tensor(st[1][:, NG - 1, :], st[1][:, NG - 1, :], st[0][:, NG - 1, :], ALU.add).then_inc(shared_done, 1)

            def apply_gate(T, p):
                pool.wait_ge(evac_done, T + 1)
                pool.wait_ge(hi_done, T + 1)
                nc.gpsimd.tensor_tensor(dx[p][:], dx[p][:], sg[p][:], ALU.mult).then_inc(yg_done, 1)

            pool.wait_ge(loaded, 16 * LOADS)
            pool.wait_ge(setup_v, SETUP_V)
            start_set(0)
            pool.wait_ge(set_step, 2)
            for q in range(4):
                convolve(f"first{q}", q, 0, None)
            pool.wait_ge(late_loaded, 16 * LATE_LOADS)
            mean(0, 1, None)
            inverse_std(0)
            affine(0, 0)
            skip_term(0, 0, 1, None)
            low_part(0, 0)
            norm(0)
            convolve("xrA.1", 0, 1, None)
            convolve("xrB.1", 1, 1, None)
            with pool.Fori(0, SETS) as s:
                with pool.Fori(0, CPS) as k:
                    c = s * CPS + k
                    for j in range(TPC):
                        T = 2 * c + j
                        U = T + 1
                        f = c + 1 + j
                        q = 2 - 2 * j
                        apply_gate(T, 1 - j)
                        mean(U, j, c)
                        inverse_std(U)
                        if j == 1:
                            with pool.If(k == CPS - 2):
                                pool.wait_ge(conv_done, 4 * c + 8)
                                pool.wait_ge(te_loaded, 16 * (s + 1))
                                start_set(s + 1)
                                pool.wait_ge(set_step, 2 * s + 4)
                                apart(pool)
                        affine(U, 1 - j)
                        skip_term(U, 1 - j, j, c)
                        split_yt(T, j, c)
                        norm(U)
                        low_part(U, 1 - j)
                        convolve(f"xrA.{j}", q, f, c)
                        if j == 1:
                            add_state(c)
                        convolve(f"xrB.{j}", q + 1, f, c)
            apply_gate(TILES, 1)
            split_yt(TILES, 0, CHUNKS)

        @block.vector
        def _(dve):
            def projections(U, j, c):
                bank, before = bank_use(f"xq.{j}", c)
                dve.wait_ge(rstd_done, U + 1)
                nc.vector.scalar_tensor_tensor(t48[:], s1[:], nmr[:], s2[:], ALU.mult, ALU.add).then_inc(x3_step, 1)
                dve.wait_ge(x3_step, 4 * U + 1)
                apart(dve)
                dve.wait_ge(*filled(f"xq.{j}", c))
                nc.vector.scalar_tensor_tensor(t48[:], wb[bank][:, 0:NPROJ], rstd[:], t48[:], ALU.mult, ALU.add).then_inc(x3_step, 1)
                dve.wait_ge(x3_step, 4 * U + 2)
                nc.vector.scalar_tensor_tensor(q48[:], wb[bank][:, PROJ:PROJ + NPROJ], rstd[:], t48[:], ALU.mult, ALU.add)\
                    .then_inc(q_done, 1)
                dve.wait_ge(q_done, U + 1)
                dve.sem_inc(bank_free[bank], 1)

            def expand(U, j, c):
                dve.wait_ge(th_done, U + 1)
                dve.wait_ge(nrm_done, U + 1)
                dve.wait_ge(coef_done, U)
                nc.vector.tensor_tensor(ta[:], th[:], a2[:], ALU.mult).then_inc(x3_step, 1)
                m = msk[:].unsqueeze(2).to_broadcast([P, NB, DS])

                def wide(a):
                    return a.unsqueeze(1).to_broadcast([P, NB, DS])

                o = [x3[:, v, :].rearrange("p (b d) -> p b d", b=NB) for v in range(3)]
                nc.vector.scalar_tensor_tensor(o[0], wide(q48[:, 0:DS]), nrm[:], m, ALU.mult, ALU.mult)
                nc.vector.tensor_tensor(o[2], wide(q48[:, DS:2 * DS]), m, ALU.mult).then_inc(x3_step, 1)
                dve.wait_ge(x3_step, 4 * U + 4)
                nc.vector.scalar_tensor_tensor(o[1], wide(ta[:]), 1.0, m, ALU.add, ALU.mult).then_inc(x3_done, 1)

            def coefficients(U, p, j, c):
                bank, before = bank_use(f"sm.{j}", c)
                dve.wait_ge(bank_ready[bank], before + 1)
                dve.wait_ge(coef_done, U)
                n0 = 7 * U
                nc.vector.tensor_reduce(ba[:], wb[bank][:, 0:2 * P].rearrange("p (v n b) -> p v n b", v=2, b=NB),
                                        AX_X, ALU.add).then_inc(coef_step, 1)
                ad = ba[:, 1, :].rearrange("p (g t) -> p g t", g=NG)
                for t in range(TS):
                    dve.wait_ge(coef_step, n0 + t + 1)
                    prev = pcar[:] if t == 0 else pp[p][:, :, t - 1]
                    nc.vector.tensor_tensor(pp[p][:, :, t], prev, ad[:, :, t], ALU.mult).then_inc(coef_step, 1)
                dve.wait_ge(coef_step, n0 + 5)
                nc.vector.reciprocal(ip[:], pp[p][:].rearrange("p g t -> p (g t)")).then_inc(coef_step, 1)
                bank_c = wb[bank][:, 2 * P:3 * P].rearrange("p (g t b) -> p g t b", g=NG, t=TS)
                for t in range(TS):
                    ins = nc.vector.tensor_tensor(lhc[p][:, :, t, t * NB:(t + 1) * NB], bank_c[:, :, t, :],
                                                  pp[p][:, :, t:t + 1].to_broadcast([P, NG, NB]), ALU.mult)
                ins.then_inc(bank_free[bank], 1)
                dve.wait_ge(coef_step, n0 + 6)
                nc.vector.tensor_scalar(lim[p][:, 0, :], ip[:], CLIP, None, ALU.mult)
                nc.vector.tensor_scalar(lim[p][:, 1, :], ip[:], -CLIP, None, ALU.mult)
                nc.vector.tensor_tensor(bdp[p][:], ba[:, 0, :], ip[:], ALU.mult).then_inc(coef_step, 1)
                dve.wait_ge(coef_step, n0 + 7)
                nc.vector.tensor_copy(pcar[:], pp[p][:, :, TS - 1]).then_inc(coef_done, 1)

            def update(T, i, p):
                t, g = i // NG, i % NG
                col = g * TS + t
                dve.wait_ge(x_done, ITEMS * T + i + 1)
                if i == 0:
                    dve.wait_ge(coef_done, T + 1)
                if g == 0:
                    dve.wait_ge(y_done, TS * T + t - 1 + Y0)
                dve.wait_ge(clip_done, ITEMS * T + i + 1 + CLIP0 - 4)
                nc.vector.scalar_tensor_tensor(st[t % 2][:, g, :], px[i % 2][:], bdp[p][:, col:col + 1],
                                               st[1 - t % 2][:, g, :], ALU.mult, ALU.add).then_inc(upd_done, 1)

            def clip(T, i, p, c):
                t, g = i // NG, i % NG
                col = g * TS + t
                if p == 1 and i == ITEMS - 1:
                    dve.wait_ge(shared_done, c + 1)
                else:
                    dve.wait_ge(upd_done, OWN * c + ITEMS * p + i + 1 + UPD0)
                nc.vector.tensor_scalar(st[t % 2][:, g, :], st[t % 2][:, g, :], lim[p][:, 0, col:col + 1],
                                        lim[p][:, 1, col:col + 1], ALU.min, ALU.max).then_inc(clip_done, 1)

            def read_y(T, p):
                dve.wait_ge(y_done, TS * T + Y0)
                dve.wait_ge(dx_done, T + 1)
                nc.vector.tensor_tensor(dx[p][:], py[:], dx[p][:], ALU.add).then_inc(evac_done, 1)

            def add_residual(T, j, c):
                bank, before = bank_use(f"ou.{j}", c)
                dve.wait_ge(bank_ready[bank], before + 1)
                dve.wait_ge(res_loaded, 16 * (T + 1))
                nc.vector.tensor_tensor(res[:], wb[bank][:], res[:], ALU.add)\
                    .then_inc(bank_free[bank], 1)

            dve.wait_ge(loaded, 16 * LOADS)
            nc.vector.memset(st[1][:, 0, 0:P], 1.0)
            nc.vector.tensor_copy(selr[:].rearrange("p a b -> p (a b)"), sg[0][:])
            nc.vector.tensor_copy(st[1][:, 1, :].rearrange("p (k x) -> p k x", k=KI), bcol[:].unsqueeze(2).to_broadcast([P, KI, P]))\
                .then_inc(setup_v, 1)
            dve.wait_ge(setup_t, 1)
            nc.vector.memset(wxg[:, :, NPROJ:PROJ], 0.0)
            nc.vector.tensor_copy(wxg[:, :, 2 * DS:3 * DS], px[0][:, 0:KI * DS].rearrange("p (k x) -> p k x", k=KI))\
                .then_inc(setup_v, 1)
            dve.wait_ge(setup_v, 2)
            raw = st[1][:, 2, 0:KI * NPROJ].rearrange("p (k x) -> p k x", k=KI)
            nc.vector.tensor_copy(raw, wxg[:, :, 0:NPROJ]).then_inc(setup_raw, 1)
            dve.wait_ge(setup_raw, 1)
            nc.vector.tensor_tensor(wxg[:, :, 0:NPROJ], raw, gcol[:].unsqueeze(2).to_broadcast([P, KI, NPROJ]), ALU.mult).then_inc(setup_v, 1)
            dve.wait_ge(setup_t, 2)
            nc.vector.tensor_copy(s1[:], px[1][:, 0:NPROJ])
            nc.vector.tensor_tensor(s2[:], px[1][:, HALF:HALF + NPROJ], s2[:], ALU.add)
            dve.wait_ge(setup_a, 1)
            nc.vector.tensor_scalar(a2[:], a2[:], -0.01, None, ALU.mult)
            nc.vector.tensor_reduce(wsum[:], wc[:], AX_X, ALU.add)
            nc.vector.memset(st[1][:], 0.0)
            nc.vector.memset(expo[:, 0:1], -0.5)
            nc.vector.memset(expo[:, 1:2], 0.5)
            nc.vector.memset(expo[:, 2:3], -1.0 / DI)
            nc.vector.memset(dx[1][:], 0.0)
            nc.vector.memset(sg[1][:], 0.0)
            nc.vector.memset(py[:], 0.0)
            nc.vector.memset(pcar[:], 1.0)
            nc.vector.memset(lhc[0][:], 0.0)
            nc.vector.memset(lhc[1][:], 0.0).then_inc(setup_v, 1)
            dve.wait_ge(setup_v, SETUP_V)
            dve.sem_inc(clip_done, CLIP0)
            dve.sem_inc(y_done, Y0 - 1)
            dve.wait_ge(wo_rounded, 1)
            nc.vector.tensor_tensor(wo_lo[:].rearrange("p k x -> p (k x)"), st[0][:].rearrange("p a b -> p (a b)"),
                                    wo_hi[:].bitcast(F32).rearrange("p k x -> p (k x)"), ALU.subtract).then_inc(setup_raw, 1)
            dve.wait_ge(setup_raw, 2)
            nc.vector.memset(st[0][:], 0.0).then_inc(upd_done, UPD0)

            projections(0, 1, None)
            expand(0, 1, None)
            coefficients(0, 0, 1, None)
            with dve.Fori(0, SETS) as s:
                with dve.Fori(0, CPS) as k:
                    c = s * CPS + k
                    with dve.If(k == 0):
                        dve.wait_ge(y_done, 2 * TS * c + Y0)
                        nc.vector.memset(st[1][:], 0.0).then_inc(state_zero, 1)
                        dve.wait_ge(state_zero, s + 1)
                        apart(dve)
                    for j in range(TPC):
                        T = 2 * c + j
                        U = T + 1
                        for i in range(ITEMS):
                            if i == 3:
                                read_y(T, 1 - j)
                            if i == 9:
                                projections(U, j, c)
                            if i == 12:
                                expand(U, j, c)
                            if i == 15:
                                if j == 1:
                                    with dve.If(k == CPS - 1):
                                        dve.wait_ge(coef_done, U)
                                        nc.vector.memset(pcar[:], 1.0).then_inc(decay_reset, 1)
                                        dve.wait_ge(decay_reset, s + 1)
                                        apart(dve)
                                coefficients(U, 1 - j, j, c)
                            if j == 0 or i < ITEMS - 1:
                                update(T, i, j)
                            if i >= 1:
                                clip(T, i - 1, j, c)
                        add_residual(T, j, c)
                        clip(T, ITEMS - 1, j, c)
            read_y(TILES, 1)
            add_residual(TILES, 0, CHUNKS)


SETUP_V = 4


def kernel(x, cond_2048, L0_cond_W_in, L0_cond_W_conv, L0_cond_b_conv, L0_cond_ln_g, L0_cond_ln_b, L0_cond_W_xproj,
           L0_cond_W_dt, L0_cond_b_dt, L0_cond_A_log, L0_cond_D, L0_cond_W_out):
    import numpy as np
    import concourse.bacc as bacc
    from concourse.bass_utils import run_bass_kernel_spmd

    def cols(v):
        return np.ascontiguousarray(np.asarray(v).reshape(KI, P).T)

    def rows(v, n=P):
        return np.ascontiguousarray(np.broadcast_to(np.asarray(v), (n, np.asarray(v).shape[0])))

    x = np.asarray(x)
    tiles = x.reshape(SETS, NG, NB, CPS, TPC, TS, DM).transpose(0, 3, 4, 1, 5, 2, 6).reshape(TILES, P, DM)
    xT = np.zeros((CHUNKS + 2, P, KD, CH), np.float32)
    xT[:CHUNKS] = tiles.reshape(CHUNKS, CH, KD, P).transpose(0, 3, 2, 1)
    xtok = np.zeros((TILES + 1, P, DM), np.float32)
    xtok[1:] = tiles
    temb = np.zeros((SETS + 2, P, KI, BSET), np.float32)
    temb[:SETS] = np.asarray(cond_2048).reshape(SETS, BSET, KI, P).transpose(0, 3, 2, 1)
    w_x = np.asarray(L0_cond_W_xproj)
    b_dt = np.zeros((P, NPROJ), np.float32)
    b_dt[:, 2 * DS:] = np.asarray(L0_cond_b_dt)
    row = np.arange(P)
    sel = np.zeros((P, 2 * TS, NB, DS), np.float32)
    sel[row, (row % 64) // NB, row % NB, :] = 1.0
    mask = np.zeros((P, NB), np.float32)
    mask[row, row % NB] = 1.0
    arrays = {
        "xT": xT, "xtok": xtok, "temb": temb,
        "w_in": np.ascontiguousarray(np.asarray(L0_cond_W_in).T.reshape(KD, P, 2 * DI).transpose(1, 0, 2)),
        "w_conv": np.ascontiguousarray(np.asarray(L0_cond_W_conv).reshape(KI, P, TAPS).transpose(1, 0, 2)),
        "b_conv": cols(L0_cond_b_conv), "ln_g": cols(L0_cond_ln_g), "ln_b": cols(L0_cond_ln_b),
        "g_rows": rows(L0_cond_ln_g), "b_rows": rows(L0_cond_ln_b), "d_rows": rows(L0_cond_D),
        "w_x": np.ascontiguousarray(w_x.T.reshape(KI, P, NPROJ).transpose(1, 0, 2)),
        "w_x3": np.ascontiguousarray(w_x[2 * DS:]),
        "w_dt": np.ascontiguousarray(np.asarray(L0_cond_W_dt).T),
        "b_dt": b_dt, "a_log": rows(L0_cond_A_log),
        "w_out": np.ascontiguousarray(np.asarray(L0_cond_W_out).T.reshape(KI, P, DM).transpose(1, 0, 2)),
        "ident": np.eye(P, dtype=np.float32), "sel": sel.reshape(P, 2 * TS, P), "mask": mask,
    }
    nc = bacc.Bacc("TRN2", target_bir_lowering=False, num_devices=1, dynamic_dma_scratch_size=1024)
    aps = [nc.dram_tensor(f"in_{n}", a.shape, mybir.dt.from_np(a.dtype), kind="ExternalInput").ap() for n, a in arrays.items()]
    order = dict(zip(arrays, aps))
    result = nc.dram_tensor("out", (TILES + 1, P, DM), F32, kind="ExternalOutput").ap()
    build(nc, out=result, **order)
    r = run_bass_kernel_spmd(nc, [{f"in_{n}": a for n, a in arrays.items()}], core_ids=[0])
    got = r.results[0]["out"]
    return np.ascontiguousarray(
        got[1:].reshape(SETS, CPS, TPC, NG, TS, NB, DM).transpose(0, 3, 5, 1, 2, 4, 6).reshape(BATCH, SEQ, DM))
```
